# Optimizing a Trainium2 kernel written in Bass

```python
import numpy as np
import jax
import jax.numpy as jnp

def _softmax(x, axis=-1):
    return jax.nn.softmax(x, axis=axis)

def _gelu(x):
    return jax.nn.gelu(x, approximate=True)

def _silu(x):
    return jax.nn.silu(x)

def _sigmoid(x):
    return jax.nn.sigmoid(x)

def _layernorm(x, axis=-1, eps=1e-05):
    m = jnp.mean(x, axis=axis, keepdims=True)
    v = jnp.var(x, axis=axis, keepdims=True)
    return (x - m) / jnp.sqrt(v + eps)

def _scatter_add(tgt, idx, src, axis=0):
    return tgt.at[idx].add(src)

def _segment_sum(src, seg, n):
    return jax.ops.segment_sum(src, seg, n)
kernel_name = 'mk_gnn_preln_d4_gnn_r8_b4024a'

def setup_inputs(seed: int=0):
    np.random.seed(seed)
    _w = jnp.asarray

    def _rec_inputs():
        import jax
        import jax.numpy as jnp
        _gk = jax.random.key(seed)
        x = -0.0005121 + 1.001 * jax.random.normal(jax.random.fold_in(_gk, 1), (12500, 64), jnp.float32)
        _s = jax.random.randint(jax.random.fold_in(_gk, 2), (200000,), 0, 12500, jnp.int32)
        _d = jax.random.randint(jax.random.fold_in(_gk, 3), (200000,), 0, 12500, jnp.int32)
        _loop = jnp.arange(12500, dtype=jnp.int32)
        src = jnp.concatenate([_s, _d, _loop])
        dst = jnp.concatenate([_d, _s, _loop])
        _o = jnp.argsort(dst, stable=True)
        src = src[_o]
        dst = dst[_o]
        edge_attr_64 = -2.25437e-05 + 0.999858 * jax.random.normal(jax.random.fold_in(_gk, 12), (412500, 64), jnp.float32)
        edge_type_8 = jax.random.randint(jax.random.fold_in(_gk, 14), (412500,), 0, 8, jnp.int32)
        edge_weight1 = jax.random.uniform(jax.random.fold_in(_gk, 15), (412500, 1), jnp.float32, 0.0, 0.999998)
        return (x, src, dst, edge_attr_64, edge_type_8, edge_weight1)
    x, src, dst, edge_attr_64, edge_type_8, edge_weight1 = _rec_inputs()

    def _L0_gnn_setup():
        import jax, jax.numpy as jnp
        import numpy as np
        N, E, R, H = (6250, 100000, 8, 4)
        F_IN, HID, OUT = (64, 64, 64)
        NEG_SLOPE = 0.2

        def _glorot(key, shape):
            fan_in, fan_out = (shape[-2], shape[-1])
            std = np.sqrt(2.0 / (fan_in + fan_out)).astype(np.float32)
            return jax.random.normal(key, shape, dtype=jnp.float32) * std

        def _rgat_conv(x, src, dst, etype, W, Q, K, b):
            n = x.shape[0]
            hc = W.shape[-1]
            xw = jnp.einsum('ni,rio->rno', x, W)
            qn = jnp.einsum('rno,roh->rnh', xw, Q)
            kn = jnp.einsum('rno,roh->rnh', xw, K)
            alpha = jax.nn.leaky_relu(qn[etype, dst] + kn[etype, src], NEG_SLOPE)
            amax = jax.ops.segment_max(alpha, dst, num_segments=n)
            amax = jnp.where(jnp.isfinite(amax), amax, 0.0)
            ex = jnp.exp(alpha - amax[dst])
            denom = jax.ops.segment_sum(ex, dst, num_segments=n)
            attn = ex / (denom[dst] + 1e-16)
            out_j = xw[etype, src].reshape(-1, H, hc // H)
            agg = jax.ops.segment_sum(attn[:, :, None] * out_j, dst, num_segments=n)
            return agg.reshape(n, hc) + b
        key = jax.random.key(seed)
        ks = jax.random.split(key, 12)
        x = jax.random.normal(ks[0], (N, F_IN), dtype=jnp.float32)
        adj_t = jax.random.randint(ks[1], (2, E), 0, N, dtype=jnp.int32)
        edge_types = jax.random.randint(ks[2], (E,), 0, R, dtype=jnp.int32)
        W1 = _glorot(ks[3], (R, F_IN, HID))
        Q1 = _glorot(ks[4], (R, HID, H))
        K1 = _glorot(ks[5], (R, HID, H))
        b1 = jnp.zeros((HID,), jnp.float32)
        W2 = _glorot(ks[6], (R, HID, OUT))
        Q2 = _glorot(ks[7], (R, OUT, H))
        K2 = _glorot(ks[8], (R, OUT, H))
        b2 = jnp.zeros((OUT,), jnp.float32)
        return dict(x=x, adj_t=adj_t, edge_types=edge_types, W1=W1, Q1=Q1, K1=K1, b1=b1, W2=W2, Q2=Q2, K2=K2, b2=b2)
    _L0_gnn_all = _L0_gnn_setup()
    _L0_gnn_in = {k: v for k, v in _L0_gnn_all.items() if k in ('W1', 'Q1', 'K1', 'b1', 'W2', 'Q2', 'K2', 'b2')}
    del _L0_gnn_all

    def _L1_gnn_setup():
        import jax, jax.numpy as jnp
        import numpy as np
        ALPHA = 0.2
        key = jax.random.key(seed)
        k1, k2, k3, k4 = jax.random.split(key, 4)
        N, E, d_in, d_out = (12500, 200000, 64, 64)
        node_features = jax.random.normal(k1, (N, d_in), dtype=jnp.float32)
        edge_index = jax.random.randint(k2, (2, E), 0, N, dtype=jnp.int64)
        W = jax.random.normal(k3, (d_in, d_out), dtype=jnp.float32) * (1.414 * np.sqrt(2.0 / (d_in + d_out)))
        a = jax.random.normal(k4, (2 * d_out,), dtype=jnp.float32) * (1.414 * np.sqrt(2.0 / (2 * d_out + 1)))
        return {'node_features': node_features, 'edge_index': edge_index, 'W': W, 'a': a}
    _L1_gnn_all = _L1_gnn_setup()
    _L1_gnn_in = {k: v for k, v in _L1_gnn_all.items() if k in ('W', 'a')}
    del _L1_gnn_all

    def _L2_gnn_setup():
        import jax, jax.numpy as jnp
        import numpy as np
        N_NODES = 12500
        N_EDGES = 200000
        IN_FEAT = 64
        OUT_FEAT = 64
        NUM_RELS = 8
        NUM_BASES = 4
        key = jax.random.key(seed)
        ks = jax.random.split(key, 7)
        x = jax.random.normal(ks[0], (N_NODES, IN_FEAT), dtype=jnp.float32)
        src = jax.random.randint(ks[1], (N_EDGES,), 0, N_NODES, dtype=jnp.int32)
        dst = jax.random.randint(ks[2], (N_EDGES,), 0, N_NODES, dtype=jnp.int32)
        etypes = jax.random.randint(ks[3], (N_EDGES,), 0, NUM_RELS, dtype=jnp.int32)
        norm = jax.random.uniform(ks[4], (N_EDGES, 1), dtype=jnp.float32)
        limit_w = float(np.sqrt(2.0) * np.sqrt(6.0 / (IN_FEAT + OUT_FEAT)))
        weight = jax.random.uniform(ks[5], (NUM_BASES, IN_FEAT, OUT_FEAT), dtype=jnp.float32, minval=-limit_w, maxval=limit_w)
        limit_c = float(np.sqrt(2.0) * np.sqrt(6.0 / (NUM_RELS + NUM_BASES)))
        w_comp = jax.random.uniform(ks[6], (NUM_RELS, NUM_BASES), dtype=jnp.float32, minval=-limit_c, maxval=limit_c)
        h_bias = jnp.zeros((OUT_FEAT,), dtype=jnp.float32)
        return {'x': x, 'weight': weight, 'w_comp': w_comp, 'h_bias': h_bias, 'norm': norm, 'src': src, 'dst': dst, 'etypes': etypes}
    _L2_gnn_all = _L2_gnn_setup()
    _L2_gnn_in = {k: v for k, v in _L2_gnn_all.items() if k in ('weight', 'w_comp', 'h_bias')}
    del _L2_gnn_all

    def _L3_gnn_setup():
        import jax, jax.numpy as jnp
        import numpy as np
        LN_EPS = 1e-05
        key = jax.random.key(seed)
        ks = jax.random.split(key, 8)
        N, E, D = (12500, 125000, 64)
        node_feats = jax.random.normal(ks[0], (N, D), dtype=jnp.float32)
        edge_feats = jax.random.normal(ks[1], (E, D), dtype=jnp.float32)
        edge_index = jax.random.randint(ks[2], (2, E), 0, N, dtype=jnp.int64)
        W1 = jax.random.normal(ks[3], (D, 2 * D), dtype=jnp.float32) / np.sqrt(D)
        b1 = jnp.zeros((2 * D,), dtype=jnp.float32)
        ln_g = jnp.ones((2 * D,), dtype=jnp.float32)
        ln_b = jnp.zeros((2 * D,), dtype=jnp.float32)
        W2 = jax.random.normal(ks[4], (2 * D, D), dtype=jnp.float32) / np.sqrt(2 * D)
        b2 = jnp.zeros((D,), dtype=jnp.float32)
        eps = jnp.zeros((1,), dtype=jnp.float32)
        return {'node_feats': node_feats, 'edge_feats': edge_feats, 'W1': W1, 'b1': b1, 'ln_g': ln_g, 'ln_b': ln_b, 'W2': W2, 'b2': b2, 'eps': eps, 'edge_index': edge_index, 'num_nodes': 12500}
    _L3_gnn_all = _L3_gnn_setup()
    _L3_gnn_in = {k: v for k, v in _L3_gnn_all.items() if k in ('W1', 'b1', 'ln_g', 'ln_b', 'W2', 'b2', 'eps')}
    del _L3_gnn_all
    return {'x': x, 'src': src, 'dst': dst, 'edge_attr_64': edge_attr_64, 'edge_type_8': edge_type_8, 'edge_weight1': edge_weight1, 'L0_gnn_W1': _L0_gnn_in['W1'], 'L0_gnn_Q1': _L0_gnn_in['Q1'], 'L0_gnn_K1': _L0_gnn_in['K1'], 'L0_gnn_b1': _L0_gnn_in['b1'], 'L0_gnn_W2': _L0_gnn_in['W2'], 'L0_gnn_Q2': _L0_gnn_in['Q2'], 'L0_gnn_K2': _L0_gnn_in['K2'], 'L0_gnn_b2': _L0_gnn_in['b2'], 'L1_gnn_W': _L1_gnn_in['W'], 'L1_gnn_a': _L1_gnn_in['a'], 'L2_gnn_weight': _L2_gnn_in['weight'], 'L2_gnn_w_comp': _L2_gnn_in['w_comp'], 'L2_gnn_h_bias': _L2_gnn_in['h_bias'], 'L3_gnn_W1': _L3_gnn_in['W1'], 'L3_gnn_b1': _L3_gnn_in['b1'], 'L3_gnn_ln_g': _L3_gnn_in['ln_g'], 'L3_gnn_ln_b': _L3_gnn_in['ln_b'], 'L3_gnn_W2': _L3_gnn_in['W2'], 'L3_gnn_b2': _L3_gnn_in['b2'], 'L3_gnn_eps': _L3_gnn_in['eps']}

def reference(x, src, dst, edge_attr_64, edge_type_8, edge_weight1, L0_gnn_W1, L0_gnn_Q1, L0_gnn_K1, L0_gnn_b1, L0_gnn_W2, L0_gnn_Q2, L0_gnn_K2, L0_gnn_b2, L1_gnn_W, L1_gnn_a, L2_gnn_weight, L2_gnn_w_comp, L2_gnn_h_bias, L3_gnn_W1, L3_gnn_b1, L3_gnn_ln_g, L3_gnn_ln_b, L3_gnn_W2, L3_gnn_b2, L3_gnn_eps):
    import jax
    import jax.numpy as jnp

    def _L0_gnn_ref(x, adj_t, edge_types, W1, Q1, K1, b1, W2, Q2, K2, b2):
        import jax, jax.numpy as jnp
        import numpy as np
        N, E, R, H = (6250, 100000, 8, 4)
        F_IN, HID, OUT = (64, 64, 64)
        NEG_SLOPE = 0.2

        def _glorot(key, shape):
            fan_in, fan_out = (shape[-2], shape[-1])
            std = np.sqrt(2.0 / (fan_in + fan_out)).astype(np.float32)
            return jax.random.normal(key, shape, dtype=jnp.float32) * std

        def _rgat_conv(x, src, dst, etype, W, Q, K, b):
            n = x.shape[0]
            hc = W.shape[-1]
            xw = jnp.einsum('ni,rio->rno', x, W)
            qn = jnp.einsum('rno,roh->rnh', xw, Q)
            kn = jnp.einsum('rno,roh->rnh', xw, K)
            alpha = jax.nn.leaky_relu(qn[etype, dst] + kn[etype, src], NEG_SLOPE)
            amax = jax.ops.segment_max(alpha, dst, num_segments=n)
            amax = jnp.where(jnp.isfinite(amax), amax, 0.0)
            ex = jnp.exp(alpha - amax[dst])
            denom = jax.ops.segment_sum(ex, dst, num_segments=n)
            attn = ex / (denom[dst] + 1e-16)
            out_j = xw[etype, src].reshape(-1, H, hc // H)
            agg = jax.ops.segment_sum(attn[:, :, None] * out_j, dst, num_segments=n)
            return agg.reshape(n, hc) + b
        src, dst = (adj_t[0], adj_t[1])
        h = _rgat_conv(x, src, dst, edge_types, W1, Q1, K1, b1)
        h = jax.nn.relu(h)
        return _rgat_conv(h, src, dst, edge_types, W2, Q2, K2, b2)

    def _L1_gnn_ref(node_features, edge_index, W, a):
        import jax, jax.numpy as jnp
        import numpy as np
        ALPHA = 0.2
        N = node_features.shape[0]
        d_out = W.shape[1]
        src, tgt = (edge_index[0], edge_index[1])
        h = node_features @ W
        s_src = h @ a[:d_out]
        s_tgt = h @ a[d_out:]
        e = jax.nn.leaky_relu(s_src[src] + s_tgt[tgt], negative_slope=ALPHA)
        m = jax.ops.segment_max(e, tgt, num_segments=N)
        e_exp = jnp.exp(e - m[tgt])
        denom = jax.ops.segment_sum(e_exp, tgt, num_segments=N)
        attention = e_exp / denom[tgt]
        h_prime = jax.ops.segment_sum(h[src] * attention[:, None], tgt, num_segments=N)
        return jax.nn.elu(h_prime)

    def _L2_gnn_ref(x, weight, w_comp, h_bias, norm, src, dst, etypes):
        import jax, jax.numpy as jnp
        import numpy as np
        N_NODES = 12500
        N_EDGES = 200000
        IN_FEAT = 64
        OUT_FEAT = 64
        NUM_RELS = 8
        NUM_BASES = 4
        rel_w = jnp.einsum('rb,bio->rio', w_comp, weight)
        xw = jnp.einsum('ni,rio->rno', x, rel_w)
        msg = xw[etypes, src] * norm
        node_repr = jax.ops.segment_sum(msg, dst, num_segments=x.shape[0])
        node_repr = node_repr + h_bias
        return jax.nn.relu(node_repr)

    def _L3_gnn_ref(node_feats, edge_feats, W1, b1, ln_g, ln_b, W2, b2, eps, edge_index, num_nodes):
        import jax, jax.numpy as jnp
        import numpy as np
        LN_EPS = 1e-05
        message = jax.nn.relu(node_feats[edge_index[1]] + edge_feats)
        message_reduce = jax.ops.segment_sum(message, edge_index[0], num_segments=num_nodes)
        h = (1.0 + eps) * node_feats + message_reduce
        x = h @ W1 + b1
        mu = jnp.mean(x, axis=-1, keepdims=True)
        var = jnp.mean(jnp.square(x - mu), axis=-1, keepdims=True)
        x = (x - mu) * jax.lax.rsqrt(var + LN_EPS) * ln_g + ln_b
        x = jax.nn.relu(x)
        return x @ W2 + b2
    edge_index = jnp.stack([src, dst])
    h = jnp.maximum(_layernorm(x, axis=-1), 0.0)
    x = x + _L0_gnn_ref(h, edge_index, edge_type_8, L0_gnn_W1, L0_gnn_Q1, L0_gnn_K1, L0_gnn_b1, L0_gnn_W2, L0_gnn_Q2, L0_gnn_K2, L0_gnn_b2)
    h = jnp.maximum(_layernorm(x, axis=-1), 0.0)
    x = x + _L1_gnn_ref(h, edge_index, L1_gnn_W, L1_gnn_a)
    h = jnp.maximum(_layernorm(x, axis=-1), 0.0)
    x = x + _L2_gnn_ref(h, L2_gnn_weight, L2_gnn_w_comp, L2_gnn_h_bias, edge_weight1, src, dst, edge_type_8)
    h = jnp.maximum(_layernorm(x, axis=-1), 0.0)
    x = x + _L3_gnn_ref(h, edge_attr_64, L3_gnn_W1, L3_gnn_b1, L3_gnn_ln_g, L3_gnn_ln_b, L3_gnn_W2, L3_gnn_b2, L3_gnn_eps, edge_index, 12500)
    return x

_drawn_inputs = setup_inputs


def setup_inputs(seed=0):
    import zlib

    import numpy as np

    out = dict(_drawn_inputs(seed))
    spreads = {'L0_gnn_b1': (0.0, 0.34),
     'L0_gnn_b2': (0.0, 0.1),
     'L2_gnn_h_bias': (0.0, 0.441),
     'L3_gnn_b1': (0.0, 0.8),
     'L3_gnn_ln_g': (1.0, 0.2),
     'L3_gnn_ln_b': (0.0, 0.359),
     'L3_gnn_b2': (0.0, 0.276)}
    factors = {'L0_gnn_Q1': 2.853, 'L0_gnn_K1': 3.231, 'L0_gnn_Q2': 4.276, 'L0_gnn_K2': 6.165}
    for name, (base, spread) in spreads.items():
        noise = np.random.default_rng([zlib.crc32(name.encode()), seed]).standard_normal(out[name].shape)
        drawn = base * np.exp(spread * noise) if base else spread * noise
        out[name] = jnp.asarray(drawn.astype(out[name].dtype))
    for name, factor in factors.items():
        out[name] = (out[name] * factor).astype(out[name].dtype)
    return out
```

```python
from contextlib import ExitStack, contextmanager

import numpy as np
import concourse.bass as bass
import concourse.mybir as mybir
from concourse.alu_op_type import AluOpType as ALU

F32 = mybir.dt.float32
I32 = mybir.dt.int32
BF16 = mybir.dt.bfloat16
ACT = mybir.ActivationFunctionType
AX = mybir.AxisListType.X

P = 128
N = 12500
E = 412500
D = 64
REL = 8
HEADS = 4
NT = -(-N // P)
NP = NT * P
J = 62
CH = 52
EPP = J * CH
EP = EPP * P
SUB = 104
NSUB = EPP // SUB
assert EP >= E and EPP % SUB == 0 and CH % 2 == 0
BIG = 1.0e30
FAR = 1.0e6
LN_EPS = 1e-5
SLOPE = 0.2
GT = 14
GP = GT // 2
TURNS = NT // GT
assert TURNS * GT == NT

CONV1, CONV2, GAT, RGCN, GINE = range(5)
REL_OF = [REL, REL, 1, REL, 1]
HEADS_OF = [HEADS, HEADS, 1, 0, 0]
LAYERS = range(5)
SUMMED = (CONV1, CONV2, GAT, RGCN)
GROUP = 4
SETS = 2
ACCS = GROUP * SETS
NG = -(-J // GROUP)
ACC_ROWS = NP + P
assert NG % SETS == 0


def row_in(l):
    return D + HEADS_OF[l]


def row_out(l):
    return D + 2 * HEADS_OF[l]


def q_cols(l):
    return REL_OF[l] * HEADS_OF[l]


class Steps:

    def __init__(self, eng, sem):
        self.eng, self.sem, self.base, self.n, self.whole = eng, sem, 0, 0, 0

    def done(self, instruction):
        instruction.then_inc(self.sem, 1)
        self.n += 1
        self.whole += 1

    def settle(self):
        self.eng.wait_ge(self.sem, self.base + self.n)

    @contextmanager
    def loop(self, turns, per):
        before = self.base + self.n
        with self.eng.Fori(0, turns) as turn:
            self.base, self.n = turn * per + before, 0
            yield turn
            assert self.n == per, (self.n, per)
        self.base, self.n = before + turns * per, 0


def bc(ap, axis, n):
    out = ap.unsqueeze(axis)
    shape = list(out.shape)
    shape[axis] = n
    return out.to_broadcast(shape)


def build(nc, a, out):
    ctx = ExitStack()
    with ctx:
        ctx.enter_context(nc.allow_non_contiguous_dma(reason="a few columns of one number for each partition"))

        def sb(name, shape, dt=F32):
            return ctx.enter_context(nc.sbuf_tensor(name, shape, dt))

        def sem(name):
            return ctx.enter_context(nc.semaphore(name))

        def dram(name, shape, dt=F32):
            return nc.dram_tensor(name, shape, dt, kind="Internal").ap()

        dst_f = dram("dst_f", (P * NSUB, SUB))
        sub_last = dram("sub_last", (P, NSUB))
        counts = dram("counts", (NP + 1, 1))
        tables = {l: dram(f"table{l}", (NP * REL_OF[l], row_in(l))) for l in LAYERS}
        q_node = {l: dram(f"q_node{l}", (NP, q_cols(l))) for l in (CONV1, CONV2, GAT)}
        q_rel = dram("q_rel", (EP, REL * HEADS))
        q_one = dram("q_one", (EP, 1))
        q_edge = {CONV1: q_rel, CONV2: q_rel, GAT: q_one}
        h_edge = dram("h_edge", (EP, D))
        zeros_d = dram("zeros_d", (P, J * D))
        acc = [dram(f"acc{k}", (ACC_ROWS, D)) for k in range(ACCS)]
        sums = {l: dram(f"sums{l}", (EP, row_out(l))) for l in SUMMED}

        X = sb("X", [P, NT, D])
        src1 = sb("src1", [P, EPP + 2 * J], I32)
        src8 = sb("src8", [P, EPP + 2 * J], I32)
        rel = sb("rel", [P, EPP], BF16)
        cont = sb("cont", [P, EPP])
        end_i = sb("end_i", [P, NT], I32)
        start_i = sb("start_i", [P, NT], I32)
        mask = sb("mask", [P, NT])
        cont_all = sb("cont_all", [P, 1])
        first_node = sb("first_node", [P, 1], I32)
        fix_i = sb("fix_i", [P, 1], I32)
        cont_t = sb("cont_t", [P, P])
        neg_t = sb("neg_t", [P, P])
        neg0 = sb("neg0", [P, 1])
        ident = sb("ident", [P, P])
        lower = sb("lower", [P, P], BF16)
        idle = sb("idle", [P, 1])
        idle_i = sb("idle_i", [P, 1], I32)
        iota_r = sb("iota_r", [P, REL])
        idx = sb("idx", [P, 2, J], I32)
        w_raw = sb("w_raw", [P, REL, D])
        kq = sb("kq", [D, REL, 2 * HEADS])
        w_all = sb("w_all", [P, REL * (D + 2 * HEADS)])
        w_comp = sb("w_comp", [P, REL * 4])
        bias = sb("bias", [P, 3 * D])
        wide = sb("wide", [P, 5, 2 * D])
        eps1 = sb("eps1", [P, 1])
        q_init = sb("q_init", [P, REL * HEADS])
        st = sb("st", [P, 4, NT])

        R = 31580
        region = sb("region", [P, R])

        def cut(at, *shape, dt=None):
            n = int(np.prod(shape))
            assert at + n <= R, (at, n)
            v = region[:, at:at + n]
            if dt is not None:
                v = v.bitcast(dt)
            if len(shape) == 2:
                v = v.rearrange("p (a b) -> p a b", a=shape[0])
            elif len(shape) == 3:
                v = v.rearrange("p (a b c) -> p a b c", a=shape[0], b=shape[1])
            return v

        XI, XO = 2 * J * (D + HEADS), 2 * J * (D + 2 * HEADS)
        at_q = XI + XO
        at_s = at_q + 4 * J * REL * HEADS
        dst_i = cut(0, EPP, dt=I32)
        dst_v = cut(EPP, EPP)
        rel_i = cut(2 * EPP, EPP, dt=I32)
        far_j = cut(3 * EPP, EPP)
        prev = cut(4 * EPP, 2)
        prev_i = cut(4 * EPP + 2, 1, dt=I32)
        last_b = cut(4 * EPP + 4, P)
        sub_v = cut(4 * EPP + 4 + P, NSUB)
        node_i = cut(4 * EPP + 200, NT, dt=I32)
        iota_i = cut(4 * EPP + 300, REL, dt=I32)
        j_i = cut(5 * EPP, EPP, dt=I32)
        cont_b = cut(6 * EPP, P)
        edge0_i = cut(6 * EPP + P, 1, dt=I32)
        edge0 = cut(6 * EPP + P + 1, 1)
        zeros = cut(28250, SUB * REL * HEADS)
        cmp_top = cut(0, NT, P)
        got_mid = cut(NT * P, NT, NSUB)
        got_low = cut(16000, NT, SUB)
        ix = cut(27000, 8, NT)
        ix_i = cut(28000, 2, NT, dt=I32)
        w_t = cut(28500, REL, P)[0:D]
        got = {l: cut(0, NT, row_out(l)) for l in SUMMED}
        HC = cut(7056, NT, D)
        h_s = cut(7056, GT, D)
        Y = cut(7952, GT, D)
        SQ = cut(8848, GT, D)
        EL = cut(9744, GT, D)
        DN = cut(10640, GT, HEADS)
        H = cut(13328, NT, D)
        Qn = cut(19600, NT * REL * HEADS)
        stage = cut(22736, GP, 2, REL * (D + HEADS))
        h_t = cut(30352, GP, P)
        HE = cut(0, 2, J, D)
        XS = cut(2 * J * D, 2, J, D)
        EA = cut(4 * J * D, J, D)
        MSG = cut(5 * J * D, 2, J, D)
        SAME = cut(7 * J * D, 2, GROUP, P)
        src_f = cut(7 * J * D + 2 * GROUP * P, 2, J)
        h_ini = cut(7 * J * D + 2 * GROUP * P + 2 * J, D)
        first_f = cut(at_q + 4000, 2, J)
        before = cut(at_q + 4200, J)
        other = cut(at_q + 4300, J)
        junk = cut(at_q + 4400, J, P)
        acc_v = cut(19600, NT, D)
        acc_w = cut(0, NT, D)
        xw = cut(0, GT, 2 * D)
        xsq = cut(GT * 2 * D, GT, 2 * D)
        xt = cut(2 * GT * 2 * D, GT, P)
        cm = cut(at_s + 2100, P + 1)
        ca = cut(at_s + 2100 + 132, P + 1)
        ex_c = cut(at_s + 2100 + 264, 2, P)
        e_m = cut(at_s + 2100 + 520, D + HEADS)
        e_a = cut(at_s + 2100 + 588, D + HEADS)
        fx = cut(at_s + 2100 + 656, D + 2 * HEADS)
        min_c = cut(at_s + 2100 + 728, D + HEADS)
        fac = cut(at_s + 2100 + 796, 2, D + HEADS)
        mt_c = cut(at_s + 2100 + 932, D + HEADS)
        ca_b = cut(at_s + 2100 + 1000, D + HEADS)

        ps = ctx.enter_context(nc.psum_tensor("ps", [P, 8, 512], F32))

        zeroed = sem("zeroed")
        zeros_out = sem("zeros_out")
        loaded = sem("loaded")
        prev_in = sem("prev_in")
        ident_z = sem("ident_z")
        consts = sem("consts")
        memsets = sem("memsets")
        v = sem("v_steps")
        act_s = sem("act_steps")
        search = sem("search")
        top_in = sem("top_in")
        top_out = sem("top_out")
        idx_dram = sem("idx_dram")
        mid_in = sem("mid_in")
        low_in = sem("low_in")
        dst_ready = sem("dst_ready")
        cnt_ready = sem("cnt_ready")
        cnt_out = sem("cnt_out")
        cnt_in = sem("cnt_in")
        index_done = sem("index_done")

        w_in = sem("w_in")
        w_free = sem("w_free")
        wt_ps = sem("wt_ps")
        wt_sb = sem("wt_sb")
        kq_ps = sem("kq_ps")
        w_done = sem("w_done")
        x_final = sem("x_final")
        h_ready = sem("h_ready")
        u_ready = sem("u_ready")
        var_in = sem("var_in")
        std_out = sem("std_out")
        h_copied = sem("h_copied")
        pair_t = sem("pair_t")
        pair_c = sem("pair_c")
        tile_mm = sem("tile_mm")
        free_a = sem("free_a")
        stored = [sem(f"stored{q}") for q in range(GP)]
        qn_out = sem("qn_out")
        q_scat = sem("q_scat")
        qi_in = sem("qi_in")
        table_out = sem("table_out")

        idx_ready = sem("idx_ready")
        gathered = {l: [sem(f"gathered{l}_{b}") for b in range(2)] for l in SUMMED}
        chunk_begun = sem("chunk_begun")
        ew_free = sem("ew_free")
        e_free = sem("e_free")
        e_in = [sem(f"e_in{b}") for b in range(2)]
        ew_in = sem("ew_in")
        ex_in = sem("ex_in")
        ex_out = sem("ex_out")
        sum_ready = sem("sum_ready")
        sum_out = [sem(f"sum_out{b}") for b in range(2)]
        tail = sem("tail")
        tail_t = sem("tail_t")
        carry = sem("carry")
        carry_t = sem("carry_t")
        cex_in = sem("cex_in")
        cex_out = sem("cex_out")
        fx_in = sem("fx_in")
        fx_ready = sem("fx_ready")
        fx_out = sem("fx_out")
        ends_in = [sem(f"ends_in{k}") for k in range(2)]
        ends_ready = sem("ends_ready")
        elu_in = sem("elu_in")
        elu_out = sem("elu_out")
        big_zero = sem("big_zero")
        zd_out = sem("zd_out")
        src_f_ready = sem("src_f_ready")
        rows_t = sem("rows_t")
        rows_used = sem("rows_used")
        m_done = sem("m_done")
        m_copied = sem("m_copied")
        msg_free = sem("msg_free")
        h_scat = sem("h_scat")
        hi_in = sem("hi_in")
        he_in = [sem(f"he_in{b}") for b in range(2)]
        he_free = sem("he_free")
        ea_in = sem("ea_in")
        ea_free = sem("ea_free")
        xs_in = sem("xs_in")
        xs_ready = sem("xs_ready")
        scat = [sem(f"scat{k}") for k in range(SETS)]
        acc_in = [sem(f"acc_in{k}") for k in range(2)]
        acc_free = sem("acc_free")
        hc_in = sem("hc_in")
        u_t = sem("u_t")
        u_c = sem("u_c")
        xw_ps = sem("xw_ps")
        xw_c = sem("xw_c")
        xn_ready = sem("xn_ready")
        xn_t = sem("xn_t")
        xn_c = sem("xn_c")
        y_ps = sem("y_ps")
        y_done = sem("y_done")
        out_s = sem("out_s")

        SOFT = [l for l in LAYERS if HEADS_OF[l]]
        TABLED = [CONV1, CONV2, GAT, RGCN]
        W_LOADS = [4, 4, 4, 4, 8]

        def weight_loads(sp, l):
            if l in (CONV1, CONV2):
                k = str(l + 1)
                w = a["L0_gnn_W" + k].rearrange("r i o -> i r o")
                yield w_raw[0:D], w
                yield w_raw[D:P], w
                yield kq[:, :, 0:HEADS], a["L0_gnn_K" + k].rearrange("r o h -> o r h")
                yield kq[:, :, HEADS:2 * HEADS], a["L0_gnn_Q" + k].rearrange("r o h -> o r h")
            elif l == GAT:
                yield w_raw[0:D, 0, :], a["L1_gnn_W"]
                yield w_raw[D:P, 0, :], a["L1_gnn_W"]
                yield kq[:, 0, 0:1], a["L1_gnn_a"][0:D].rearrange("(o h) -> o h", h=1)
                yield kq[:, 0, 1:2], a["L1_gnn_a"][D:2 * D].rearrange("(o h) -> o h", h=1)
            elif l == RGCN:
                w = a["L2_gnn_weight"].rearrange("b i o -> i b o")
                yield w_raw[0:D, 0:4, :], w
                yield w_raw[D:P, 0:4, :], w
                yield w_comp[:, :], a["L2_gnn_w_comp"].rearrange("r b -> (r b)").partition_broadcast(P)
                yield bias[:, 2 * D:3 * D], a["L2_gnn_h_bias"].partition_broadcast(P)
            else:
                yield wide[0:D, 3, :], a["L3_gnn_W1"]
                yield wide[D:P, 3, :], a["L3_gnn_W1"]
                yield wide[:, 4, 0:D], a["L3_gnn_W2"]
                yield wide[:, 4, D:2 * D], a["L3_gnn_b2"].partition_broadcast(P)
                yield wide[:, 0, :], a["L3_gnn_b1"].partition_broadcast(P)
                yield wide[:, 1, :], a["L3_gnn_ln_g"].partition_broadcast(P)
                yield wide[:, 2, :], a["L3_gnn_ln_b"].partition_broadcast(P)
                yield eps1[:, :], a["L3_gnn_eps"].partition_broadcast(P)

        def w_loaded(l):
            return 16 * sum(W_LOADS[:l + 1])

        ZEROS = NSUB + 1 + 2 + 2 * ACCS

        def set_tiles(k):
            return sum(min(GROUP, J - GROUP * n) for n in range(k, NG, SETS))

        def slots(l):
            h = HEADS_OF[l]
            ri, ro = row_in(l), row_out(l)
            G = cut(0, 2, J, ri)
            O = cut(XI, 2, J, ro)
            return h, G, O

        block = ctx.enter_context(nc.Block())

        @block.sync
        def _(sp):
            part = lambda x: x.rearrange("(p j) -> p j", p=P)
            sp.dma_start(dst_i, part(a["dst"])).then_inc(loaded, 16)
            sp.dma_start(src1[:, 0:EPP], part(a["src"])).then_inc(loaded, 16)
            sp.dma_start(rel_i, part(a["edge_type_8"])).then_inc(loaded, 16)
            sp.dma_start(X[:, :, :], a["x"].rearrange("(p t) d -> p t d", p=P)).then_inc(loaded, 16)
            sp.dma_start(bias[:, 0:D], a["L0_gnn_b1"].partition_broadcast(P)).then_inc(loaded, 16)
            sp.dma_start(bias[:, D:2 * D], a["L0_gnn_b2"].partition_broadcast(P)).then_inc(loaded, 16)
            sp.wait_ge(memsets, 1)
            sp.dma_start(prev_i[1:P, :], part(a["dst"])[0:P - 1, EPP - 1:EPP]).then_inc(prev_in, 16)
            for l in (CONV1,):
                for to, of in weight_loads(sp, l):
                    sp.dma_start(to, of).then_inc(w_in, 16)
            sp.wait_ge(dst_ready, 1)
            sp.dma_start(dst_f.rearrange("(p s) k -> p (s k)", p=P), dst_v).then_inc(idx_dram, 16)
            sp.dma_start(sub_last, sub_v).then_inc(idx_dram, 16)
            sp.wait_ge(cnt_ready, 1)
            sp.dma_start(counts[1:NP + 1, :].rearrange("(p t) k -> p (t k)", p=P), ix[:, 5, :]).then_inc(cnt_out, 16)
            sp.dma_start(counts[0:1, :], ix[0:1, 7, 0:1]).then_inc(cnt_out, 16)
            sp.wait_ge(cnt_out, 32)
            sp.dma_start(ix[:, 6, :], counts[0:NP, :].rearrange("(p t) k -> p (t k)", p=P)).then_inc(cnt_in, 16)

            for l in LAYERS:
                if l in TABLED:
                    w = REL_OF[l] * row_in(l)
                    rows = tables[l].rearrange("(p t r) f -> p t (r f)", p=P, t=NT)
                    n0 = NT * l + 2
                    with sp.Fori(0, TURNS) as g:
                        for q in range(GP):
                            sp.wait_ge(free_a, g * GT + (n0 + 2 * q + 2))
                            sp.dma_start(rows[:, bass.ds(g * GT + 2 * q, 2), :], stage[:, q, :, 0:w]).then_inc(stored[q], 16)
                    if l in SOFT:
                        sp.wait_ge(free_a, NT * (l + 1) + 2)
                        k = q_cols(l)
                        sp.dma_start(q_node[l].rearrange("(p t) k -> p (t k)", p=P), Qn[:, 0:NT * k]).then_inc(qn_out, 16)
                else:
                    sp.wait_ge(h_ready, TURNS * (l + 1))
                    sp.dma_start(tables[l].rearrange("(p t) f -> p t f", p=P), H).then_inc(table_out, 16)
                if l < GINE:
                    if l in TABLED:
                        sp.wait_ge(tile_mm, NT * (l + 1))
                    for to, of in weight_loads(sp, l + 1):
                        sp.dma_start(to, of).then_inc(w_in, 16)
                if l == GINE:
                    sp.wait_ge(h_scat, 16 * NT)
                    w = J * D
                    he = h_edge.rearrange("(p j) k -> p (j k)", p=P)
                    ea = a["edge_attr_64"].rearrange("(p j) k -> p (j k)", p=P)
                    with sp.Fori(0, CH // 2) as i:
                        for b in range(2):
                            sp.wait_ge(he_free, i * 2 + (b + 1))
                            sp.dma_start(HE[:, b].rearrange("p j d -> p (j d)"),
                                         he[:, bass.ds(i * (2 * w) + b * w, w)]).then_inc(he_in[b], 16)
                            sp.wait_ge(ea_free, i * 2 + (b + 1))
                            sp.dma_start(EA.rearrange("p j d -> p (j d)"),
                                         ea[:, bass.ds(i * (2 * w) + b * w, w)]).then_inc(ea_in, 16)
                    break
                rows = sums[l].rearrange("(p j) f -> p j f", p=P)
                _, _, O = slots(l)
                with sp.Fori(0, CH // 2) as i:
                    for b in range(2):
                        sp.wait_ge(sum_ready, i * 2 + (CH * l + b + 1))
                        sp.dma_start(rows[:, bass.ds(i * (2 * J) + b * J, J), :], O[:, b]).then_inc(sum_out[b], 16)
                        if l == CONV1:
                            he = h_edge.rearrange("(p j) k -> p (j k)", p=P)
                            sp.dma_start(he[:, bass.ds(i * (2 * J * D) + b * J * D, J * D)], zeros_d).then_inc(big_zero, 16)
            for k in range(SETS):
                sp.wait_ge(scat[k], 16 * CH * set_tiles(k))
            for k in range(ACCS):
                sp.wait_ge(acc_free, k + 1)
                to = H if k == 0 else acc_v if k % 2 else acc_w
                sp.dma_start(to, acc[k][0:NP, :].rearrange("(p t) f -> p t f", p=P)).then_inc(acc_in[k % 2], 16)
            sp.dma_start(HC, tables[GINE].rearrange("(p t) f -> p t f", p=P)).then_inc(hc_in, 16)
            rows = out.rearrange("(p t) d -> p t d", p=P)
            with sp.Fori(0, TURNS) as g:
                sp.wait_ge(y_done, g + 1)
                sp.dma_start(rows[:, bass.ds(g * GT, GT), :], X[:, bass.ds(g * GT, GT), :]).then_inc(out_s, 16)
            sp.wait_ge(out_s, 16 * TURNS)

        @block.gpsimd
        def _(pool):
            def gather(to, table, index, s):
                pool.indirect_dma_start(out=to, out_offset=None, in_=table,
                                        in_offset=bass.IndirectOffsetOnAxis(ap=index, axis=0)).then_inc(s, 16)

            pool.memset(ident[:, :], 0.0).then_inc(ident_z, 1)
            pool.wait_ge(ident_z, 1)
            pool.affine_select(out=ident[:, :], in_=ident[:, :], compare_op=ALU.not_equal, fill=1.0, base=0,
                               pattern=[[-1, P]], channel_multiplier=1).then_inc(consts, 1)
            pool.iota(node_i, pattern=[[1, NT]], base=0, channel_multiplier=NT).then_inc(consts, 1)
            pool.iota(iota_i, pattern=[[1, REL]], base=0, channel_multiplier=0).then_inc(consts, 1)
            pool.iota(j_i, pattern=[[1, EPP]], base=-1, channel_multiplier=0).then_inc(consts, 1)

            pool.iota(idle_i[:, :], pattern=[[1, 1]], base=NP, channel_multiplier=1).then_inc(consts, 1)
            pool.memset(lower[:, :], 1.0).then_inc(ident_z, 1)
            pool.wait_ge(ident_z, 2)
            pool.affine_select(out=lower[:, :], in_=lower[:, :], compare_op=ALU.is_gt, fill=0.0, base=0,
                               pattern=[[-1, P]], channel_multiplier=1).then_inc(consts, 1)
            pool.iota(edge0_i, pattern=[[1, 1]], base=0, channel_multiplier=EPP).then_inc(consts, 1)
            pool.wait_ge(idx_dram, 32)
            pool.wait_ge(search, 1)
            for t in range(NT):
                gather(got_mid[:, t, :], sub_last, ix_i[:, 0, t:t + 1], mid_in)
            pool.wait_ge(search, 2)
            for t in range(NT):
                gather(got_low[:, t, :], dst_f, ix_i[:, 1, t:t + 1], low_in)
            pool.wait_ge(index_done, 1)
            pool.wait_ge(zeros_out, 16 * ZEROS)

            for l in LAYERS:
                if l in SOFT:
                    k = q_cols(l)
                    for t in range(NT):
                        if t % GT == 0:
                            pool.wait_ge(free_a, NT * l + t + GT + 2)
                        pool.indirect_dma_start(
                            out=q_edge[l], out_offset=bass.IndirectOffsetOnAxis(ap=start_i[:, t:t + 1], axis=0),
                            in_=Qn[:, t * k:(t + 1) * k], in_offset=None,
                            bounds_check=EP - 1, oob_is_err=False).then_inc(q_scat, 16)
                    pool.wait_ge(qn_out, 16 * (l + 1))
                    gather(q_init[:, 0:k], q_node[l], first_node[:, 0:1], qi_in)
                if l == GINE:
                    pool.wait_ge(big_zero, 16 * CH)
                    for t in range(NT):
                        if t % GT == 0:
                            pool.wait_ge(h_ready, TURNS * l + t // GT + 1)
                        pool.indirect_dma_start(
                            out=h_edge, out_offset=bass.IndirectOffsetOnAxis(ap=start_i[:, t:t + 1], axis=0),
                            in_=H[:, t, :], in_offset=None,
                            bounds_check=EP - 1, oob_is_err=False).then_inc(h_scat, 16)
                    pool.wait_ge(table_out, 16)
                    gather(h_ini, tables[GINE], first_node[:, 0:1], hi_in)
                    with pool.Fori(0, CH // 2) as i:
                        for b in range(2):
                            pool.wait_ge(idx_ready, i * 2 + ((CH + 2) * len(SUMMED) + b + 1))
                            pool.sem_inc(chunk_begun, 1)
                            for n in range(NG):
                                k, before_n = n % SETS, GROUP * (n // SETS)
                                pool.wait_ge(m_copied, i * (2 * NG) + (NG * b + n + 3))
                                pool.sem_inc(chunk_begun, 1)
                                pool.wait_ge(scat[k], i * (32 * set_tiles(k)) + 16 * (set_tiles(k) * b + before_n))
                                pool.sem_inc(msg_free if n == SETS - 1 else chunk_begun, 1)
                                for j in range(GROUP * n, min(GROUP * (n + 1), J)):
                                    pool.indirect_dma_start(
                                        out=acc[GROUP * k + j % GROUP],
                                        out_offset=bass.IndirectOffsetOnAxis(ap=idx[:, b, j:j + 1], axis=0),
                                        in_=MSG[:, b, j, :], in_offset=None, compute_op=ALU.add).then_inc(scat[k], 16)
                    break
                for q in range(GP):
                    pool.wait_ge(stored[q], 16 * TURNS * (l + 1))
                _, G, _ = slots(l)
                with pool.Fori(0, CH // 2) as i:
                    for b in range(2):
                        pool.wait_ge(idx_ready, i * 2 + ((CH + 2) * l + b + 1))
                        pool.sem_inc(chunk_begun, 1)
                        for j in range(J):
                            gather(G[:, b, j, :], tables[l], idx[:, b, j:j + 1], gathered[l][b])
                for b in range(2):
                    pool.wait_ge(sum_out[b], 16 * (CH // 2) * (l + 1))
                gather(fx[:, 0:row_out(l)], sums[l], fix_i[:, 0:1], fx_in)
                pool.wait_ge(fx_ready, l + 1)
                pool.indirect_dma_start(
                    out=sums[l], out_offset=bass.IndirectOffsetOnAxis(ap=fix_i[:, 0:1], axis=0),
                    in_=fx[:, 0:row_out(l)], in_offset=None).then_inc(fx_out, 16)
                pool.wait_ge(fx_out, 16 * (l + 1))
                for g in range(TURNS + 1):
                    if g < TURNS:
                        for t in range(GT * g, GT * (g + 1)):
                            gather(got[l][:, t, :], sums[l], end_i[:, t:t + 1], ends_in[g % 2])
                    if g:
                        k = (g - 1) % 2
                        landed = (TURNS + 1 - k) // 2 * l + (g - 1) // 2 + 1
                        pool.wait_ge(ends_in[k], 16 * GT * landed)
                        pool.sem_inc(ends_ready, 1)
            pool.wait_ge(u_ready, 1)
            with pool.Fori(0, TURNS) as g:
                pool.wait_ge(u_t, g)
                pool.tensor_copy(h_s, H[:, bass.ds(g * GT, GT), :]).then_inc(h_copied, 1)

        @block.scalar
        def _(act):
            steps = Steps(act, act_s)
            act.sem_inc(free_a, 2)
            act.sem_inc(m_copied, 2)
            act.wait_ge(zeroed, 1)
            rows = q_rel.rearrange("(p s j) k -> p s (j k)", p=P, s=NSUB)
            for s in range(NSUB):
                act.dma_start(rows[:, s, :], zeros).then_inc(zeros_out, 16)
            act.dma_start(q_one.rearrange("(p j) k -> p (j k)", p=P), zeros[:, 0:EPP]).then_inc(zeros_out, 16)

            for c in range(2):
                act.dma_start(zeros_d[:, c * J * D // 2:(c + 1) * J * D // 2], zeros[:, 0:J * D // 2]).then_inc(zeros_out, 16)
            w = ACC_ROWS // P * D // 2
            for k in range(ACCS):
                for c in range(2):
                    act.dma_start(acc[k].rearrange("(p t) f -> p (t f)", p=P)[:, c * w:(c + 1) * w],
                                  zeros[:, 0:w]).then_inc(zeros_out, 16)

            def std(n):
                act.wait_ge(var_in, n)
                act.activation(st[:, 2, 0:GT], st[:, 1, 0:GT], ACT.Sqrt).then_inc(std_out, 1)

            for l in LAYERS:
                if l == CONV1:
                    act.wait_ge(zeros_out, 16 * ZEROS)
                w, k = REL_OF[l] * row_in(l), q_cols(l)
                half = w // 2 if REL_OF[l] > 1 else w
                qn = Qn[:, 0:NT * k].rearrange("p (t k) -> p t k", t=NT) if k else None
                with act.Fori(0, TURNS) as g:
                    def copy_pair(q):
                        act.wait_ge(pair_t, g * GP + (GP * TURNS * l + q + 1))
                        act.copy(h_t[:, q, :], ps[:, q % 2, 0:P]).then_inc(pair_c, 1)

                    if l == RGCN:
                        act.wait_ge(elu_in, g + 1)
                        act.activation(EL, EL, ACT.Exp).then_inc(elu_out, 1)
                    if l != CONV2:
                        std(g + TURNS * {CONV1: 0, GAT: 1, RGCN: 2, GINE: 3}[l] + 1)
                    if l in TABLED:
                        copy_pair(0)
                        for q in range(GP):
                            if q + 1 < GP:
                                copy_pair(q + 1)
                            act.wait_ge(stored[q], g * 16 + 16 * TURNS * l)
                            for u in (2 * q, 2 * q + 1):
                                bank = 2 + 2 * (u % 2)
                                act.wait_ge(tile_mm, g * GT + (NT * l + u + 1))
                                last = act.copy(stage[:, q, u % 2, 0:half], ps[:, bank, 0:half])
                                if half < w:
                                    last = act.copy(stage[:, q, u % 2, half:w], ps[:, bank + 1, 0:w - half])
                                if k:
                                    last = act.copy(qn[:, bass.ds(g * GT + u, 1), :],
                                                    ps[:, bank + 1, w - half:w - half + k].unsqueeze(1))
                                last.then_inc(free_a, 1)
                h, _, _ = slots(l)
                if h:
                    k = q_cols(l)
                    w = J * k
                    rows = q_edge[l].rearrange("(p j) k -> p (j k)", p=P)
                    to = [cut(at_q + b * w, w) for b in range(2)]
                    nth = l
                    act.wait_ge(q_scat, 16 * NT * (l + 1))
                    ex = cut(at_s + 1000, 2 * h * J)
                    with act.Fori(0, CH // 2) as i:
                        for b in range(2):
                            act.wait_ge(e_free, i * 2 + ((CH + 2) * nth + b + 1))
                            act.dma_start(to[b], rows[:, bass.ds(i * (2 * w) + b * w, w)]).then_inc(e_in[b], 16)
                            act.wait_ge(ex_in, i * 2 + (CH * nth + b + 1))
                            act.activation(ex, ex, ACT.Exp).then_inc(ex_out, 1)
                if l == RGCN:
                    act.wait_ge(ew_free, 1)
                    act.dma_start(cut(at_q, EPP), a["edge_weight1"].rearrange("(p j) k -> p (j k)", p=P)).then_inc(ew_in, 16)
                if h:
                    act.wait_ge(cex_in, 2 * l + 1)
                    act.activation(ex_c[0:D + h], ex_c[0:D + h], ACT.Exp).then_inc(cex_out, 1)
                    act.wait_ge(cex_in, 2 * l + 2)
                    act.activation(fac[:, :, 0:D + h], fac[:, :, 0:D + h], ACT.Exp).then_inc(cex_out, 1)
            with act.Fori(0, CH // 2) as i:
                for b in range(2):
                    act.wait_ge(xs_in, i * 2 + (b + 1))
                    act.activation(XS[:, b], XS[:, b], ACT.Relu).then_inc(xs_ready, 1)
                    act.wait_ge(msg_free, i * 2 + b)
                    for n in range(NG):
                        j0, j1 = GROUP * n, min(GROUP * (n + 1), J)
                        act.wait_ge(m_done, i * (2 * NG) + (NG * b + n + 3))
                        act.copy(MSG[:, b, j0:j1, :],
                                 ps[:, 2 + n % 2, 0:(j1 - j0) * D].rearrange("p (j d) -> p j d", d=D)).then_inc(m_copied, 1)
            with act.Fori(0, TURNS) as g:
                std(g + (4 * TURNS + 1))

        @block.tensor
        def _(pe):
            def ps_pair(q):
                return ps[:, q % 2, 0:P]

            pe.sem_inc(m_done, 2)

            def source_rows(i, phase, b, n, src_b):
                pe.wait_ge(rows_used, i * (2 * NG) + (2 * NG * (CH // 2) * phase + NG * b + n + 1))
                for j in range(GROUP * n, min(GROUP * (n + 1), J)):
                    c = j % GROUP
                    last = pe.transpose(ps[:, n % 2, c * P:(c + 1) * P], src_b[:, j:j + 1].to_broadcast([P, P]), ident[:, :])
                last.then_inc(rows_t, 1)

            def prepare(l):
                h = HEADS_OF[l]
                if not h:
                    return
                pe.wait_ge(w_in, w_loaded(l))
                if l > 1:
                    pe.wait_ge(fx_ready, l - 1)
                elif l == 0:
                    pe.wait_ge(index_done, 1)
                for r in range(REL_OF[l]):
                    last = pe.transpose(ps[0:D, 6 + r // 4, (r % 4) * P:(r % 4 + 1) * P], w_raw[:, r, :], ident[:, :])
                last.then_inc(wt_ps, 1)
                pe.wait_ge(wt_sb, l + 1)
                for r in range(REL_OF[l]):
                    last = pe.matmul(ps[:, 0, r * 2 * h:(r + 1) * 2 * h], w_t[:, r, :], kq[:, r, 0:2 * h],
                                     start=True, stop=True)
                last.then_inc(kq_ps, 1)

            pe.wait_ge(consts, 7)
            pe.wait_ge(top_in, 1)
            pe.transpose(ps[:, 6, 0:P], last_b, ident[:, :]).then_inc(top_out, 1)
            pe.wait_ge(top_in, 2)
            pe.transpose(ps[:, 7, 0:P], cont_b, ident[:, :]).then_inc(top_out, 1)

            for l in LAYERS:
                h = HEADS_OF[l]
                if l == CONV1:
                    prepare(l)
                if l in TABLED:
                    w = REL_OF[l] * row_in(l)
                    half = w // 2 if REL_OF[l] > 1 else w
                    cols = w + q_cols(l)
                    pe.wait_ge(w_done, l + 1)
                    with pe.Fori(0, TURNS) as g:
                        pe.wait_ge(h_ready, g + (TURNS * l + 1))
                        def turn_pair(q):
                            pair = h_s[:, 2 * q:2 * q + 2, :].rearrange("p t d -> p (t d)")
                            pe.transpose(ps_pair(q), pair, ident[:, :]).then_inc(pair_t, 1)

                        turn_pair(0)
                        for q in range(GP):
                            if q + 1 < GP:
                                turn_pair(q + 1)
                            pe.wait_ge(pair_c, g * GP + (GP * TURNS * l + q + 1))
                            for k in range(2):
                                u = 2 * q + k
                                lo = slice(D * k, D * k + D)
                                pe.wait_ge(free_a, g * GT + (NT * l + u + 1))
                                pe.matmul(ps[:, 2 + 2 * k, 0:half], h_t[lo, q, :], w_all[lo, 0:half],
                                          start=True, stop=True)
                                last = pe.matmul(ps[:, 3 + 2 * k, 0:cols - half], h_t[lo, q, :],
                                                 w_all[lo, half:cols], start=True, stop=True)
                                last.then_inc(tile_mm, 1)
                if l + 1 in TABLED:
                    prepare(l + 1)
                if l == RGCN:
                    with pe.Fori(0, CH // 2) as i:
                        for b in range(2):
                            pe.wait_ge(src_f_ready, i * 2 + (b + 1))
                            for n in range(NG):
                                source_rows(i, 0, b, n, first_f[:, b])
                if l == GINE:
                    with pe.Fori(0, CH // 2) as i:
                        for b in range(2):
                            pe.wait_ge(src_f_ready, i * 2 + (CH + b + 1))
                            source_rows(i, 1, b, 0, src_f[:, b])
                            for n in range(NG):
                                if n + 1 < NG:
                                    source_rows(i, 1, b, n + 1, src_f[:, b])
                                if n == 0:
                                    pe.wait_ge(xs_ready, i * 2 + (b + 1))
                                pe.wait_ge(rows_used, i * (2 * NG) + (NG * CH + NG * b + n + 3))
                                pe.wait_ge(m_copied, i * (2 * NG) + (NG * b + n + 1))
                                for j in range(GROUP * n, min(GROUP * (n + 1), J)):
                                    c = j % GROUP
                                    last = pe.matmul(ps[:, 2 + n % 2, c * D:(c + 1) * D], SAME[:, n % 2, c, :],
                                                     XS[:, b, j, :], start=True, stop=True)
                                last.then_inc(m_done, 1)
                    break
                f = D + h
                pe.wait_ge(tail, l + 1)
                if h:
                    pe.transpose(ps[0:f, 6, 0:P], e_m[:, 0:f], ident[:, :])
                pe.transpose(ps[0:f, 6, P:2 * P], e_a[:, 0:f], ident[:, :]).then_inc(tail_t, 1)
                pe.wait_ge(carry, l + 1)
                if h:
                    pe.transpose(ps[:, 7, 0:f], cm[0:f, 0:P], ident[0:f, 0:f])
                pe.transpose(ps[:, 7, P:P + f], ca[0:f, 0:P], ident[0:f, 0:f]).then_inc(carry_t, 1)
            pe.wait_ge(w_in, w_loaded(GINE))
            with pe.Fori(0, TURNS) as g:
                pe.wait_ge(h_copied, g + 1)
                for q in range(GP):
                    pair = h_s[:, 2 * q:2 * q + 2, :].rearrange("p t d -> p (t d)")
                    last = pe.transpose(ps[:, q // 4, (q % 4) * P:(q % 4 + 1) * P], pair, ident[:, :])
                last.then_inc(u_t, 1)
                pe.wait_ge(u_c, g + 1)
                for u in range(GT):
                    k, q = u % 2, u // 2
                    lo = slice(D * k, D * k + D)
                    last = pe.matmul(ps[:, 2 + 2 * k + q // 4, (q % 4) * P:(q % 4 + 1) * P], h_t[lo, u // 2, :], wide[lo, 3, :],
                                     start=True, stop=True)
                last.then_inc(xw_ps, 1)
                pe.wait_ge(xn_ready, g + 1)
                for u in range(GT):
                    last = pe.transpose(ps[:, 2 + u // 4, (u % 4) * P:(u % 4 + 1) * P], xw[:, u, :], ident[:, :])
                last.then_inc(xn_t, 1)
                pe.wait_ge(xn_c, g + 1)
                for u in range(GT):
                    last = pe.matmul(ps[:, 6 + u // 8, (u % 8) * D:(u % 8 + 1) * D], xt[:, u, :], wide[:, 4, 0:D],
                                     start=True, stop=True)
                last.then_inc(y_ps, 1)

        @block.vector
        def _(dve):
            s = Steps(dve, v)
            done, settle = s.done, s.settle
            tt, ts_, stt = dve.tensor_tensor, dve.tensor_scalar, dve.scalar_tensor_tensor
            dve.sem_inc(rows_used, 2)

            dve.memset(zeros, 0.0).then_inc(zeroed, 1)
            done(dve.memset(src1[:, EPP:], 0))
            done(dve.memset(src8[:, EPP:], 0))
            done(dve.memset(ix[:, 7, :], 0.0))
            dve.memset(prev_i, -1).then_inc(memsets, 1)
            dve.wait_ge(loaded, 96)
            done(dve.tensor_copy(dst_v, dst_i))
            done(dve.tensor_copy(first_node[:, :], dst_i[:, 0:1]))
            done(dve.tensor_copy(rel[:, :], rel_i))
            done(stt(out=src8[:, 0:EPP], in0=src1[:, 0:EPP], scalar=float(REL), in1=rel_i, op0=ALU.mult, op1=ALU.add))
            dve.wait_ge(prev_in, 16)
            done(dve.tensor_copy(prev[:, 0:1], prev_i))
            settle()
            dve.tensor_copy(sub_v, dst_v[:, SUB - 1:EPP:SUB]).then_inc(dst_ready, 1)
            dve.tensor_copy(last_b, dst_v[:, EPP - 1:EPP].to_broadcast([P, P])).then_inc(top_in, 1)
            done(tt(cont[:, 1:EPP], dst_v[:, 1:EPP], dst_v[:, 0:EPP - 1], ALU.is_equal))
            done(tt(cont[:, 0:1], dst_v[:, 0:1], prev[:, 0:1], ALU.is_equal))
            dve.wait_ge(consts, 7)
            done(dve.tensor_copy(far_j, j_i))
            done(dve.tensor_copy(edge0, edge0_i))
            done(dve.tensor_copy(iota_r[:, :], iota_i))
            done(dve.tensor_copy(idle[:, :], idle_i[:, :]))
            done(dve.tensor_copy(ix[:, 0, :], node_i))
            settle()
            done(dve.tensor_reduce(cont_all[:, :], cont[:, :], AX, ALU.min))
            done(stt(out=far_j[:, 1:EPP], in0=cont[:, 1:EPP], scalar=FAR, in1=far_j[:, 1:EPP], op0=ALU.mult, op1=ALU.add))
            done(ts_(neg0[:, :], cont[:, 0:1], -1.0, BIG, ALU.add, ALU.mult))
            done(ts_(ix[:, 0, :], ix[:, 0, :], float(N - 1), None, ALU.min))
            settle()
            done(dve.tensor_reduce(prev[:, 0:1], far_j[:, 1:EPP], AX, ALU.min))
            settle()
            done(ts_(prev[:, 0:1], prev[:, 0:1], float(EPP - 1), None, ALU.min))
            settle()
            done(ts_(fix_i[:, :], prev[:, 0:1], edge0[:, 0:1], None, ALU.add))
            dve.tensor_copy(cont_b, cont_all[:, 0:1].to_broadcast([P, P])).then_inc(top_in, 1)
            dve.wait_ge(top_out, 2)
            done(dve.tensor_copy(cont_t[:, :], ps[:, 7, 0:P]))
            settle()
            done(ts_(neg_t[:, :], cont_t[:, :], -1.0, BIG, ALU.add, ALU.mult))
            dve.wait_ge(idx_dram, 32)
            dve.wait_ge(top_in, 2)
            done(tt(cmp_top, bc(ps[:, 6, 0:P], 1, NT), bc(ix[:, 0, :], 2, P), ALU.is_le))
            settle()
            done(dve.tensor_reduce(ix[:, 1, :], cmp_top, AX, ALU.add))
            settle()
            dve.tensor_copy(ix_i[:, 0, :], ix[:, 1, :]).then_inc(search, 1)
            dve.wait_ge(mid_in, 16 * NT)
            done(tt(got_mid, got_mid, bc(ix[:, 0, :], 2, NSUB), ALU.is_le))
            settle()
            done(dve.tensor_reduce(ix[:, 2, :], got_mid, AX, ALU.add))
            settle()
            done(stt(out=ix[:, 3, :], in0=ix[:, 1, :], scalar=float(NSUB), in1=ix[:, 2, :], op0=ALU.mult, op1=ALU.add))
            settle()
            dve.tensor_copy(ix_i[:, 1, :], ix[:, 3, :]).then_inc(search, 1)
            dve.wait_ge(low_in, 16 * NT)
            done(tt(got_low, got_low, bc(ix[:, 0, :], 2, SUB), ALU.is_le))
            settle()
            done(dve.tensor_reduce(ix[:, 4, :], got_low, AX, ALU.add))
            settle()
            stt(out=ix[:, 5, :], in0=ix[:, 3, :], scalar=float(SUB), in1=ix[:, 4, :], op0=ALU.mult,
                op1=ALU.add).then_inc(cnt_ready, 1)
            dve.wait_ge(cnt_ready, 1)
            dve.wait_ge(cnt_in, 16)
            done(tt(mask[:, :], ix[:, 5, :], ix[:, 6, :], ALU.is_gt))
            done(ts_(end_i[:, :], ix[:, 5, :], -1.0, 0.0, ALU.add, ALU.max))
            settle()
            done(ts_(ix[:, 4, :], mask[:, :], -FAR, FAR, ALU.mult, ALU.add))
            settle()
            tt(start_i[:, :], ix[:, 6, :], ix[:, 4, :], ALU.add).then_inc(index_done, 1)
            dve.wait_ge(index_done, 1)

            dve.wait_ge(zeros_out, 16 * ZEROS)

            def norm(src, to, sq, width, nth_std):
                mean, var, sd, rs = (st[:, k, 0:GT] for k in range(4))
                done(dve.tensor_reduce(mean, src, AX, ALU.add))
                settle()
                done(ts_(mean, mean, 1.0 / width, None, ALU.mult))
                settle()
                done(tt(to, src, bc(mean, 2, width), ALU.subtract))
                settle()
                done(tt(sq, to, to, ALU.mult))
                settle()
                done(dve.tensor_reduce(var, sq, AX, ALU.add))
                settle()
                ts_(var, var, 1.0 / width, LN_EPS, ALU.mult, ALU.add).then_inc(var_in, 1)
                dve.wait_ge(std_out, nth_std)
                done(dve.reciprocal(rs, sd))
                settle()
                return rs

            def weights(l):
                h = HEADS_OF[l]
                ri, k, rels = row_in(l), q_cols(l), REL_OF[l]
                w = rels * ri
                dve.wait_ge(w_in, w_loaded(l))
                if h:
                    dve.wait_ge(wt_ps, l + 1)
                    for r0 in range(0, rels, 4):
                        n = min(4, rels - r0)
                        last = dve.tensor_copy(w_t[:, r0:r0 + n, :],
                                               ps[0:D, 6 + r0 // 4, 0:n * P].rearrange("p (r i) -> p r i", r=n))
                    last.then_inc(wt_sb, 1)
                    tab = w_all[:, 0:w].rearrange("p (r f) -> p r f", r=rels)
                    done(dve.tensor_copy(tab[:, :, 0:D], w_raw[:, 0:rels, :]))
                    dve.wait_ge(kq_ps, l + 1)
                    both = ps[:, 0, 0:rels * 2 * h].rearrange("p (r f) -> p r f", r=rels)
                    done(dve.tensor_copy(tab[:, :, D:ri], both[:, :, 0:h]))
                    dve.tensor_copy(w_all[:, w:w + k].rearrange("p (r f) -> p r f", r=rels),
                                    both[:, :, h:2 * h]).then_inc(w_done, 1)
                else:
                    for r in range(rels):
                        o = w_all[:, r * D:(r + 1) * D]
                        done(ts_(o, w_raw[:, 0, :], w_comp[:, 4 * r:4 * r + 1], None, ALU.mult))
                    for b in range(1, 4):
                        settle()
                        for r in range(rels):
                            o = w_all[:, r * D:(r + 1) * D]
                            last = stt(out=o, in0=w_raw[:, b, :], scalar=w_comp[:, 4 * r + b:4 * r + b + 1], in1=o,
                                       op0=ALU.mult, op1=ALU.add)
                            if (b, r) != (3, rels - 1):
                                done(last)
                    last.then_inc(w_done, 1)

            def result(l, g):
                h = HEADS_OF[l]
                tiles = bass.ds(g * GT, GT)
                xg, mk = X[:, tiles, :], mask[:, tiles]
                dve.wait_ge(ends_ready, g + (TURNS * l + 1))
                if h:
                    den = DN[:, :, 0:h]
                    done(ts_(den, got[l][:, tiles, D:D + h], 0.0 if l == GAT else 1e-16, None, ALU.add))
                    settle()
                    done(dve.reciprocal(den, den))
                    settle()
                    done(tt(den, den, bc(mk, 2, h), ALU.mult))
                    settle()
                    w = D // h
                    for hh in range(h):
                        last = tt(Y[:, :, hh * w:(hh + 1) * w], got[l][:, tiles, hh * w:(hh + 1) * w],
                                  bc(den[:, :, hh], 2, w), ALU.mult)
                    done(last)
                else:
                    done(tt(Y, got[l][:, tiles, 0:D], bc(mk, 2, D), ALU.mult))
                settle()
                if l == CONV1:
                    done(tt(Y, Y, bc(bias[:, 0:D], 1, GT), ALU.add))
                    settle()
                    dve.wait_ge(pair_t, g * GP + GP * TURNS * (l + 1))
                    ts_(h_s, Y, 0.0, None, ALU.max).then_inc(h_ready, 1)
                elif l == CONV2:
                    done(tt(Y, Y, bc(bias[:, D:2 * D], 1, GT), ALU.add))
                    settle()
                    done(tt(xg, xg, Y, ALU.add))
                elif l == GAT:
                    ts_(EL, Y, 0.0, None, ALU.min).then_inc(elu_in, 1)
                    dve.wait_ge(elu_out, g + 1)
                    done(stt(out=Y, in0=Y, scalar=0.0, in1=EL, op0=ALU.max, op1=ALU.add))
                    settle()
                    done(stt(out=xg, in0=Y, scalar=-1.0, in1=xg, op0=ALU.add, op1=ALU.add))
                else:
                    done(tt(Y, Y, bc(bias[:, 2 * D:3 * D], 1, GT), ALU.add))
                    settle()
                    done(stt(out=xg, in0=Y, scalar=0.0, in1=xg, op0=ALU.max, op1=ALU.add))
                settle()

            def gine_edges():
                dve.sem_inc(he_free, 2)
                dve.sem_inc(ea_free, 1)
                dve.wait_ge(hi_in, 16)
                with s.loop(CH // 2, 2) as i:
                    for b in range(2):
                        at = i * (2 * J) + b * J
                        cj = cont[:, bass.ds(at, J)]
                        dve.wait_ge(msg_free, i * 2 + b)
                        dve.tensor_copy(src_f[:, b, :], src1[:, bass.ds(at, J)]).then_inc(src_f_ready, 1)
                        dve.tensor_copy(idx[:, b, :], src8[:, bass.ds(at, J)]).then_inc(idx_ready, 1)
                        dve.wait_ge(he_in[b], i * 16 + 16)
                        for f in range(D):
                            last = dve.tensor_tensor_scan(XS[:, b, :, f], cj, HE[:, b, :, f], h_ini[:, f:f + 1],
                                                          ALU.mult, ALU.add)
                        last.then_inc(he_free, 1)
                        dve.wait_ge(he_free, i * 2 + (b + 3))
                        done(dve.tensor_copy(h_ini, XS[:, b, J - 1, :]))
                        settle()
                        dve.wait_ge(ea_in, i * 32 + 16 * (b + 1))
                        tt(XS[:, b], XS[:, b], EA, ALU.add).then_inc(xs_in, 1)
                        dve.wait_ge(xs_in, i * 2 + (b + 1))
                        dve.sem_inc(ea_free, 1)
                        for n in range(NG):
                            j0, j1 = GROUP * n, min(GROUP * (n + 1), J)
                            dve.wait_ge(rows_t, i * (2 * NG) + (NG * CH + NG * b + n + 1))
                            dve.wait_ge(m_done, i * (2 * NG) + (NG * b + n + 1))
                            tt(SAME[:, n % 2, 0:j1 - j0, :],
                               ps[:, n % 2, 0:(j1 - j0) * P].rearrange("p (j i) -> p j i", i=P),
                               bc(src_f[:, b, j0:j1], 2, P), ALU.is_equal).then_inc(rows_used, 1)

            def gine_nodes():
                for k in range(SETS):
                    dve.wait_ge(scat[k], 16 * CH * set_tiles(k))
                dve.sem_inc(acc_free, 3)
                dve.wait_ge(acc_in[0], 16)
                for k in range(1, ACCS):
                    dve.wait_ge(acc_in[k % 2], 16 * (k // 2 + 1))
                    tt(H, H, acc_v if k % 2 else acc_w, ALU.add).then_inc(acc_free, 1)
                    dve.wait_ge(acc_free, k + 3)
                dve.wait_ge(hc_in, 16)
                done(ts_(eps1[:, :], eps1[:, :], 1.0, None, ALU.add))
                settle()
                stt(out=H, in0=HC, scalar=eps1[:, 0:1], in1=H, op0=ALU.mult, op1=ALU.add).then_inc(u_ready, 1)

            for l in LAYERS:
                h, G, O = slots(l)
                ri, ro, k = row_in(l), row_out(l), q_cols(l)
                rels = REL_OF[l]
                w = rels * ri
                if l == CONV1:
                    weights(l)
                nth_ln = {CONV1: 0, CONV2: 0, GAT: 1, RGCN: 2, GINE: 3}[l]
                with s.loop(TURNS, {CONV1: 6, CONV2: 5, GAT: 12, RGCN: 12, GINE: 9}[l]) as g:
                    if l:
                        result(l - 1, g)
                    if l != CONV2:
                        dve.sem_inc(x_final, 1)
                        rs = norm(X[:, bass.ds(g * GT, GT), :], Y, SQ, D, g + (TURNS * nth_ln + 1))
                        if l in TABLED:
                            dve.wait_ge(pair_t, g * GP + GP * TURNS * l)
                            to = h_s
                        else:
                            to = H[:, bass.ds(g * GT, GT), :]
                        stt(out=to, in0=Y, scalar=0.0, in1=bc(rs, 2, D), op0=ALU.max, op1=ALU.mult).then_inc(h_ready, 1)
                    dve.wait_ge(h_ready, g + (TURNS * l + 1))
                if l in TABLED:
                    for q in range(GP):
                        dve.wait_ge(stored[q], 16 * TURNS * (l + 1))
                    dve.wait_ge(free_a, NT * (l + 1) + 2)
                else:
                    dve.wait_ge(table_out, 16)
                    dve.wait_ge(h_scat, 16 * NT)
                    gine_edges()
                    gine_nodes()
                    break
                if h:
                    dve.wait_ge(q_scat, 16 * NT * (l + 1))
                    dve.wait_ge(qn_out, 16 * (l + 1))
                    dve.wait_ge(qi_in, 16 * (l + 1))
                which = src8 if rels > 1 else src1
                nth = l
                ew = cut(at_q, EPP)
                if l == RGCN:
                    dve.sem_inc(ew_free, 1)
                for b in range(2):
                    dve.tensor_copy(idx[:, b, :], which[:, b * J:(b + 1) * J]).then_inc(idx_ready, 1)
                done(dve.memset(O[:, 1, J - 1, :], 0.0))
                if h:
                    dve.sem_inc(e_free, 2)
                    w_e = J * k
                    EQ = [cut(at_q + b * w_e, J, k) for b in range(2)]
                    QX = cut(at_q + 2 * w_e, J, k)
                    TM = cut(at_q + 3 * w_e, J, k)
                    OH = cut(at_s, J, REL)
                    Q = cut(at_s + 500, h, J)
                    M = cut(at_s + 1500, 2, h, J + 1)
                    EX = cut(at_s + 1000, 2, h, J)
                    NEG = cut(at_s + 2010, J)
                    done(dve.memset(M[:, 1, :, J:J + 1], -BIG))
                    done(dve.tensor_copy(QX[:, J - 1, :], q_init[:, 0:k]))
                if l + 1 in TABLED:
                    weights(l + 1)
                if l == RGCN:
                    dve.wait_ge(ew_in, 16)
                per = {CONV1: 24, CONV2: 24, GAT: 18, RGCN: 10}[l]
                settle()
                with s.loop(CH // 2, per) as i:
                    for b in range(2):
                        at = i * (2 * J) + b * J
                        cj = cont[:, bass.ds(at, J)]
                        ob = 1 - b
                        if h:
                            dve.wait_ge(e_in[b], i * 16 + 16 * (CH // 2) * nth + 16)
                            for c in range(k):
                                last = dve.tensor_tensor_scan(TM[:, :, c], cj, EQ[b][:, :, c], QX[:, J - 1, c:c + 1],
                                                              ALU.mult, ALU.add)
                            last.then_inc(e_free, 1)
                            dve.wait_ge(e_free, i * 2 + ((CH + 2) * nth + b + 3))
                            done(dve.tensor_copy(QX[:, J - 1, :], TM[:, J - 1, :]))
                            done(ts_(NEG, cj, -1.0, BIG, ALU.add, ALU.mult))
                            if rels > 1:
                                done(tt(OH, bc(rel[:, bass.ds(at, J)], 2, REL), bc(iota_r[:, :], 1, J), ALU.is_equal))
                                settle()
                                tm4 = TM.rearrange("p j (r h) -> p j h r", r=rels)
                                for hh in range(h):
                                    last = tt(tm4[:, :, hh, :], tm4[:, :, hh, :], OH, ALU.mult)
                                done(last)
                                settle()
                                done(dve.tensor_reduce(Q.rearrange("p h j -> p j h"), tm4, AX, ALU.add))
                                settle()
                                qv = Q
                            else:
                                qv = TM.rearrange("p j k -> p k j")
                                settle()
                            dve.wait_ge(gathered[l][b], i * (16 * J) + 16 * J)
                            done(tt(Q, qv, G[:, b, :, D:ri].rearrange("p j h -> p h j"), ALU.add))
                            settle()
                            done(stt(out=Q, in0=Q, scalar=SLOPE, in1=Q, op0=ALU.mult, op1=ALU.max))
                            done(dve.tensor_copy(M[:, b, :, 0:1], M[:, ob, :, J:J + 1]))
                            settle()
                            for hh in range(h):
                                last = dve.tensor_tensor_scan(M[:, b, hh, 1:J + 1], NEG, Q[:, hh, :],
                                                              M[:, b, hh, 0:1], ALU.add, ALU.max)
                            done(last)
                            settle()
                            done(tt(EX[:, 0], M[:, b, :, 0:J], M[:, b, :, 1:J + 1], ALU.subtract))
                            settle()
                            done(tt(EX[:, 0], EX[:, 0], bc(NEG, 1, h), ALU.add))
                            tt(EX[:, 1], Q, M[:, b, :, 1:J + 1], ALU.subtract).then_inc(ex_in, 1)
                            dve.wait_ge(ex_out, i * 2 + (CH * nth + b + 1))
                            gh = G[:, b, :, 0:D].rearrange("p j (h f) -> p j h f", h=h)
                            for hh in range(h):
                                last = tt(gh[:, :, hh, :], gh[:, :, hh, :], bc(EX[:, 1, hh, :], 2, D // h), ALU.mult)
                            done(last)
                        else:
                            dve.tensor_copy(first_f[:, b, :], src1[:, bass.ds(at, J)]).then_inc(src_f_ready, 1)
                            for n in range(NG):
                                dve.wait_ge(rows_t, i * (2 * NG) + (NG * b + n + 1))
                                for j in range(GROUP * n, min(GROUP * (n + 1), J)):
                                    c = j % GROUP
                                    last = stt(out=junk[:, j, :], in0=ps[:, n % 2, c * P:(c + 1) * P],
                                               scalar=first_f[:, b, j:j + 1], in1=lower[:, :], op0=ALU.is_equal,
                                               op1=ALU.mult, accum_out=before[:, j:j + 1])
                                last.then_inc(rows_used, 1)
                            dve.wait_ge(rows_used, i * (2 * NG) + (NG * b + NG + 2))
                            done(ts_(before, before, 1.0, None, ALU.min))
                            done(ts_(other, first_f[:, b, :], -1.0, idle[:, 0:1], ALU.mult, ALU.add))
                            settle()
                            done(tt(other, other, before, ALU.mult))
                            settle()
                            done(tt(src8[:, bass.ds(at, J)], other, first_f[:, b, :], ALU.add))
                            dve.wait_ge(gathered[l][b], i * (16 * J) + 16 * J)
                            g_b = G[:, b, :, :]
                            done(tt(g_b, g_b, bc(ew[:, bass.ds(at, J)], 2, D), ALU.mult))
                        settle()
                        dve.wait_ge(sum_out[b], i * 16 + 16 * (CH // 2) * l)
                        for f in range(D):
                            fac_j = EX[:, 0, f * h // D, :] if h else cj
                            last = dve.tensor_tensor_scan(O[:, b, :, f], fac_j, G[:, b, :, f], O[:, ob, J - 1, f:f + 1],
                                                          ALU.mult, ALU.add)
                        if h:
                            for hh in range(h):
                                dve.tensor_tensor_scan(O[:, b, :, D + hh], EX[:, 0, hh, :], EX[:, 1, hh, :],
                                                       O[:, ob, J - 1, D + hh:D + hh + 1], ALU.mult, ALU.add)
                            last = dve.tensor_copy(O[:, b, :, D + h:D + 2 * h].rearrange("p j h -> p h j"),
                                                   M[:, b, :, 1:J + 1])
                        last.then_inc(sum_ready, 1)
                        dve.wait_ge(sum_ready, i * 2 + (CH * l + b + 1))
                        dve.tensor_copy(idx[:, b, :], which[:, bass.ds(at + 2 * J, J)]).then_inc(idx_ready, 1)
                f = D + h
                tail_row = O[:, 1, J - 1, :]
                if h:
                    for hh in range(h):
                        done(dve.tensor_copy(e_m[:, hh * D // h:(hh + 1) * D // h],
                                             tail_row[:, f + hh:f + hh + 1].to_broadcast([P, D // h])))
                    done(dve.tensor_copy(e_m[:, D:f], tail_row[:, f:f + h]))
                dve.tensor_copy(e_a[:, 0:f], tail_row[:, 0:f]).then_inc(tail, 1)
                if h:
                    done(dve.memset(cm[:, 0:1], -BIG))
                done(dve.memset(ca[:, 0:1], 0.0))
                dve.wait_ge(tail_t, l + 1)
                settle()
                if h:
                    done(dve.tensor_tensor_scan(cm[0:f, 1:P + 1], neg_t[0:f, :], ps[0:f, 6, 0:P], -BIG, ALU.add, ALU.max))
                    settle()
                    done(tt(ex_c[0:f, 0], cm[0:f, 0:P], cm[0:f, 1:P + 1], ALU.subtract))
                    settle()
                    done(tt(ex_c[0:f, 0], ex_c[0:f, 0], neg_t[0:f, :], ALU.add))
                    tt(ex_c[0:f, 1], ps[0:f, 6, 0:P], cm[0:f, 1:P + 1], ALU.subtract).then_inc(cex_in, 1)
                    dve.wait_ge(cex_out, 2 * l + 1)
                    done(tt(ex_c[0:f, 1], ex_c[0:f, 1], ps[0:f, 6, P:2 * P], ALU.mult))
                    settle()
                    dve.tensor_tensor_scan(ca[0:f, 1:P + 1], ex_c[0:f, 0], ex_c[0:f, 1], 0.0,
                                           ALU.mult, ALU.add).then_inc(carry, 1)
                else:
                    dve.tensor_tensor_scan(ca[0:f, 1:P + 1], cont_t[0:f, :], ps[0:f, 6, P:2 * P], 0.0,
                                           ALU.mult, ALU.add).then_inc(carry, 1)
                dve.wait_ge(carry_t, l + 1)
                dve.wait_ge(fx_in, 16 * (l + 1))
                if h:
                    done(ts_(min_c[:, 0:f], ps[:, 7, 0:f], neg0[:, 0:1], None, ALU.add))
                    for hh in range(h):
                        done(dve.tensor_copy(e_m[:, hh * D // h:(hh + 1) * D // h],
                                             fx[:, f + hh:f + hh + 1].to_broadcast([P, D // h])))
                    done(dve.tensor_copy(e_m[:, D:f], fx[:, f:f + h]))
                    settle()
                    done(tt(mt_c[:, 0:f], e_m[:, 0:f], min_c[:, 0:f], ALU.max))
                    settle()
                    done(tt(fac[:, 0, 0:f], e_m[:, 0:f], mt_c[:, 0:f], ALU.subtract))
                    tt(fac[:, 1, 0:f], min_c[:, 0:f], mt_c[:, 0:f], ALU.subtract).then_inc(cex_in, 1)
                    dve.wait_ge(cex_out, 2 * l + 2)
                    done(tt(fx[:, 0:f], fx[:, 0:f], fac[:, 0, 0:f], ALU.mult))
                    done(tt(ca_b[:, 0:f], ps[:, 7, P:P + f], fac[:, 1, 0:f], ALU.mult))
                    done(dve.tensor_copy(fx[:, f:f + h], mt_c[:, D:f]))
                    settle()
                    tt(fx[:, 0:f], fx[:, 0:f], ca_b[:, 0:f], ALU.add).then_inc(fx_ready, 1)
                else:
                    stt(out=fx[:, 0:D], in0=ps[:, 7, P:P + D], scalar=cont[:, 0:1], in1=fx[:, 0:D],
                        op0=ALU.mult, op1=ALU.add).then_inc(fx_ready, 1)

            XW4 = ps[:, 2:6, :].rearrange("p a (u c) -> p (a u) c", c=P)[:, 0:GT, :]
            with s.loop(TURNS, 13) as g:
                dve.wait_ge(u_t, g + 1)
                done(dve.tensor_copy(h_t[:, 0:4, :], ps[:, 0, :].rearrange("p (q c) -> p q c", q=4)))
                dve.tensor_copy(h_t[:, 4:GP, :], ps[:, 1, 0:(GP - 4) * P].rearrange("p (q c) -> p q c", c=P)).then_inc(u_c, 1)
                dve.wait_ge(xw_ps, g + 1)
                for k in range(2):
                    half_ps = ps[:, 2 + 2 * k:4 + 2 * k, :].rearrange("p a (u c) -> p (a u) c", c=P)[:, 0:GP, :]
                    last = tt(xw[:, k:GT:2, :], half_ps, bc(wide[:, 0, :], 1, GP), ALU.add)
                done(last)
                settle()
                rs = norm(xw, xw, xsq, 2 * D, g + (4 * TURNS + 1))
                done(tt(xw, xw, bc(rs, 2, 2 * D), ALU.mult))
                settle()
                done(tt(xw, xw, bc(wide[:, 1, :], 1, GT), ALU.mult))
                settle()
                done(tt(xw, xw, bc(wide[:, 2, :], 1, GT), ALU.add))
                settle()
                ts_(xw, xw, 0.0, None, ALU.max).then_inc(xn_ready, 1)
                dve.wait_ge(xn_t, g + 1)
                dve.tensor_copy(xt, XW4).then_inc(xn_c, 1)
                dve.wait_ge(y_ps, g + 1)
                xg = X[:, bass.ds(g * GT, GT), :]
                done(tt(xg, xg, bc(wide[:, 4, D:2 * D], 1, GT), ALU.add))
                settle()
                xa, xb = X[:, bass.ds(g * GT, 8), :], X[:, bass.ds(g * GT + 8, GT - 8), :]
                done(tt(xa, xa, ps[:, 6, :].rearrange("p (u c) -> p u c", c=D), ALU.add))
                tt(xb, xb, ps[:, 7, 0:(GT - 8) * D].rearrange("p (u c) -> p u c", c=D),
                   ALU.add).then_inc(y_done, 1)


_INS = ['x', 'src', 'dst', 'edge_attr_64', 'edge_type_8', 'edge_weight1', 'L0_gnn_W1', 'L0_gnn_Q1', 'L0_gnn_K1',
        'L0_gnn_b1', 'L0_gnn_W2', 'L0_gnn_Q2', 'L0_gnn_K2', 'L0_gnn_b2', 'L1_gnn_W', 'L1_gnn_a', 'L2_gnn_weight',
        'L2_gnn_w_comp', 'L2_gnn_h_bias', 'L3_gnn_W1', 'L3_gnn_b1', 'L3_gnn_ln_g', 'L3_gnn_ln_b', 'L3_gnn_W2',
        'L3_gnn_b2', 'L3_gnn_eps']


def kernel(**inputs):
    import concourse.bacc as bacc
    from concourse.bass_utils import run_bass_kernel_spmd as run

    pads = {'x': (NP, 0), 'src': (EP, 0), 'dst': (EP, N), 'edge_attr_64': (EP, 0), 'edge_type_8': (EP, 0),
            'edge_weight1': (EP, 0)}
    nc = bacc.Bacc("TRN2", target_bir_lowering=False, num_devices=1)
    arrays, args = {}, {}
    for name in _INS:
        v = np.ascontiguousarray(inputs[name])
        if name in pads:
            rows, fill = pads[name]
            v = np.concatenate([v, np.full((rows - v.shape[0],) + v.shape[1:], fill, v.dtype)])
        arrays[f"in_{name}"] = v
        args[name] = nc.dram_tensor(f"in_{name}", v.shape, mybir.dt.from_np(v.dtype), kind="ExternalInput").ap()
    out = nc.dram_tensor("out", (NP, D), F32, kind="ExternalOutput").ap()
    build(nc, args, out)
    r = run(nc, [arrays], core_ids=[0])
    return r.results[0]["out"][:N]
```

```python
from contextlib import ExitStack, contextmanager

import numpy as np
import concourse.bass as bass
import concourse.mybir as mybir
from concourse.alu_op_type import AluOpType as ALU

F32 = mybir.dt.float32
I32 = mybir.dt.int32
BF16 = mybir.dt.bfloat16
ACT = mybir.ActivationFunctionType
AX = mybir.AxisListType.X

P = 128
N = 12500
E = 412500
D = 64
REL = 8
HEADS = 4
NT = -(-N // P)
NP = NT * P
J = 62
CH = 52
EPP = J * CH
EP = EPP * P
SUB = 104
NSUB = EPP // SUB
assert EP >= E and EPP % SUB == 0 and CH % 2 == 0
BIG = 1.0e30
ZW = 496
ZREP = 8
FAR = 1.0e6
LN_EPS = 1e-5
SLOPE = 0.2
GT = 14
GP = GT // 2
TURNS = NT // GT
assert TURNS * GT == NT

CONV1, CONV2, GAT, RGCN, GINE = range(5)
REL_OF = [REL, REL, 1, REL, 1]
HEADS_OF = [HEADS, HEADS, 1, 0, 0]
LAYERS = range(5)
SUMMED = (CONV1, CONV2, GAT, RGCN)
GROUP = 4
BATCH = 2
SETS = 4
ACCS = BATCH * SETS
GC = 4
NG = -(-J // GROUP)
ACC_ROWS = NP + P
assert J % BATCH == 0 and GC * J // BATCH % SETS == 0 and CH % GC == 0


def row_in(l):
    return D + HEADS_OF[l]


def row_out(l):
    return D + 2 * HEADS_OF[l]


def q_cols(l):
    return REL_OF[l] * HEADS_OF[l]


class Steps:

    def __init__(self, eng, sem):
        self.eng, self.sem, self.base, self.n, self.whole = eng, sem, 0, 0, 0

    def done(self, instruction):
        instruction.then_inc(self.sem, 1)
        self.n += 1
        self.whole += 1

    def settle(self):
        self.eng.wait_ge(self.sem, self.base + self.n)

    @contextmanager
    def loop(self, turns, per):
        before = self.base + self.n
        with self.eng.Fori(0, turns) as turn:
            self.base, self.n = turn * per + before, 0
            yield turn
            assert self.n == per, (self.n, per)
        self.base, self.n = before + turns * per, 0


def bc(ap, axis, n):
    out = ap.unsqueeze(axis)
    shape = list(out.shape)
    shape[axis] = n
    return out.to_broadcast(shape)


def build(nc, a, out):
    ctx = ExitStack()
    with ctx:
        ctx.enter_context(nc.allow_non_contiguous_dma(reason="a few columns of one number for each partition"))

        def sb(name, shape, dt=F32):
            return ctx.enter_context(nc.sbuf_tensor(name, shape, dt))

        def sem(name):
            return ctx.enter_context(nc.semaphore(name))

        def dram(name, shape, dt=F32):
            return nc.dram_tensor(name, shape, dt, kind="Internal").ap()

        dst_f = dram("dst_f", (P * NSUB, SUB))
        sub_last = dram("sub_last", (P, NSUB))
        counts = dram("counts", (NP + 1, 1))
        tables = {l: dram(f"table{l}", (NP * REL_OF[l], row_in(l))) for l in LAYERS}
        q_node = {l: dram(f"q_node{l}", (NP, q_cols(l))) for l in (CONV1, CONV2, GAT)}
        q_rel = dram("q_rel", (EP, REL * HEADS))
        q_one = dram("q_one", (EP, 1))
        q_edge = {CONV1: q_rel, CONV2: q_rel, GAT: q_one}
        h_edge = dram("h_edge", (EP, D))
        zeros_d = dram("zeros_d", (P, J * D))
        acc = [dram(f"acc{k}", (ACC_ROWS, D)) for k in range(ACCS)]
        sums = {l: dram(f"sums{l}", (EP, row_out(l))) for l in SUMMED}

        X = sb("X", [P, NT, D])
        src1 = sb("src1", [P, EPP + 2 * J], I32)
        src8 = sb("src8", [P, EPP + 2 * J], I32)
        rel = sb("rel", [P, EPP], BF16)
        cont = sb("cont", [P, EPP])
        end_i = sb("end_i", [P, NT], I32)
        start_i = sb("start_i", [P, NT], I32)
        mask = sb("mask", [P, NT])
        cont_all = sb("cont_all", [P, 1])
        first_node = sb("first_node", [P, 1], I32)
        fix_i = sb("fix_i", [P, 1], I32)
        cont_t = sb("cont_t", [P, P])
        neg_t = sb("neg_t", [P, P])
        neg0 = sb("neg0", [P, 1])
        ident = sb("ident", [P, P])
        lower = sb("lower", [P, P], BF16)
        idle = sb("idle", [P, 1])
        idle_i = sb("idle_i", [P, 1], I32)
        iota_r = sb("iota_r", [P, REL])
        idx = sb("idx", [P, 2, J], I32)
        w_raw = sb("w_raw", [P, REL, D])
        kq = sb("kq", [D, REL, 2 * HEADS])
        w_all = sb("w_all", [P, REL * (D + 2 * HEADS)])
        w_comp = sb("w_comp", [P, REL * 4])
        bias = sb("bias", [P, 3 * D])
        wide = sb("wide", [P, 5, 2 * D])
        eps1 = sb("eps1", [P, 1])
        q_init = sb("q_init", [P, REL * HEADS])
        st = sb("st", [P, 4, NT])

        R = 31580
        region = sb("region", [P, R])

        def cut(at, *shape, dt=None):
            n = int(np.prod(shape))
            assert at + n <= R, (at, n)
            v = region[:, at:at + n]
            if dt is not None:
                v = v.bitcast(dt)
            if len(shape) == 2:
                v = v.rearrange("p (a b) -> p a b", a=shape[0])
            elif len(shape) == 3:
                v = v.rearrange("p (a b c) -> p a b c", a=shape[0], b=shape[1])
            return v

        XI, XO = 2 * J * (D + HEADS), 2 * J * (D + 2 * HEADS)
        at_q = XI + XO
        at_s = at_q + 4 * J * REL * HEADS
        dst_i = cut(0, EPP, dt=I32)
        dst_v = cut(EPP, EPP)
        zeros = cut(2 * EPP, ZW)
        far_j = cut(10700, EPP)
        cmp_top = cut(10700 + EPP, GT, P)
        got_mid = [cut(g * GT * NSUB, GT, NSUB) for g in range(TURNS)]
        got_low = [cut(10700 + g * GT * SUB if g < 5 else 3100 + (g - 5) * GT * SUB, GT, SUB) for g in range(TURNS)]
        ix = cut(17980, 8, NT)
        ix_i = cut(18764, 2, NT, dt=I32)
        last_b = cut(18960, P)
        cont_b = cut(19088, P)
        node_i = cut(19216, NT, dt=I32)
        iota_i = cut(19314, REL, dt=I32)
        sub_v = cut(19322, NSUB)
        prev = cut(19354, 2)
        prev_i = cut(19356, 1, dt=I32)
        edge0_i = cut(19357, 1, dt=I32)
        edge0 = cut(19358, 1)
        w_t = cut(28500, REL, P)[0:D]
        got = {l: cut(0, NT, row_out(l)) for l in SUMMED}
        h_s = cut(7056, GT, D)
        Y = cut(7952, GT, D)
        SQ = cut(8848, GT, D)
        EL = cut(9744, GT, D)
        DN = cut(10640, GT, HEADS)
        H = cut(13328, NT, D)
        Qn = cut(19600, NT * REL * HEADS)
        stage = cut(22736, GP, 2, REL * (D + HEADS))
        h_t = cut(30352, GP, P)
        HE = cut(0, 2, J, D)
        XS = cut(2 * J * D, 2, J, D)
        EA = cut(4 * J * D, J, D)
        MSG = cut(5 * J * D, 2, J, D)
        SAME = cut(7 * J * D, 2, GROUP, P)
        src_f = cut(7 * J * D + 2 * GROUP * P, 2, J)
        h_ini = cut(7 * J * D + 2 * GROUP * P + 2 * J, D)
        first_f = cut(at_q + 4000, 2, J)
        before = cut(at_q + 4200, J)
        other = cut(at_q + 4300, J)
        junk = cut(at_q + 4400, J, P)
        AC = cut(0, ACCS + 1, GT * D)
        at_u = (ACCS + 1) * GT * D
        U = cut(at_u, GT, D)
        xw = cut(at_u + GT * D, GT, 2 * D)
        xsq = cut(at_u + 3 * GT * D, GT, 2 * D)
        xr = cut(at_u + 5 * GT * D, GT, 2 * D)
        xt = cut(at_u + 7 * GT * D, GT, P)
        cm = cut(at_s + 2100, P + 1)
        ca = cut(at_s + 2100 + 132, P + 1)
        ex_c = cut(at_s + 2100 + 264, 2, P)
        e_m = cut(at_s + 2100 + 520, D + HEADS)
        e_a = cut(at_s + 2100 + 588, D + HEADS)
        fx = cut(at_s + 2100 + 656, D + 2 * HEADS)
        min_c = cut(at_s + 2100 + 728, D + HEADS)
        fac = cut(at_s + 2100 + 796, 2, D + HEADS)
        mt_c = cut(at_s + 2100 + 932, D + HEADS)
        ca_b = cut(at_s + 2100 + 1000, D + HEADS)

        ps = ctx.enter_context(nc.psum_tensor("ps", [P, 8, 512], F32))

        zeroed = sem("zeroed")
        zeros_out = sem("zeros_out")
        loaded = sem("loaded")
        banks_read = sem("banks_read")
        dst_in = sem("dst_in")
        prev_in = sem("prev_in")
        ident_z = sem("ident_z")
        consts = sem("consts")
        memsets = sem("memsets")
        v = sem("v_steps")
        act_s = sem("act_steps")
        search = sem("search")
        top_in = sem("top_in")
        top_out = sem("top_out")
        idx_dram = sem("idx_dram")
        mid_in = [sem(f"mid_in{g}") for g in range(TURNS)]
        low_in = [sem(f"low_in{g}") for g in range(TURNS)]
        dst_ready = sem("dst_ready")
        cnt_ready = sem("cnt_ready")
        cnt_out = sem("cnt_out")
        cnt_in = sem("cnt_in")
        index_done = sem("index_done")

        w_in = sem("w_in")
        w_free = sem("w_free")
        wt_ps = sem("wt_ps")
        wt_sb = sem("wt_sb")
        kq_ps = sem("kq_ps")
        w_done = sem("w_done")
        x_final = sem("x_final")
        h_ready = sem("h_ready")
        ac_in = sem("ac_in")
        ac_free = sem("ac_free")
        u_ready = sem("u_ready")
        var_in = sem("var_in")
        std_out = sem("std_out")
        pair_t = sem("pair_t")
        pair_c = sem("pair_c")
        tile_mm = sem("tile_mm")
        free_a = sem("free_a")
        stored = [sem(f"stored{q}") for q in range(GP)]
        qn_out = sem("qn_out")
        q_scat = sem("q_scat")
        qi_in = sem("qi_in")
        table_out = sem("table_out")

        idx_ready = sem("idx_ready")
        gathered = {l: [sem(f"gathered{l}_{b}") for b in range(2)] for l in SUMMED}
        chunk_begun = sem("chunk_begun")
        ew_free = sem("ew_free")
        e_free = sem("e_free")
        e_in = [sem(f"e_in{b}") for b in range(2)]
        ew_in = sem("ew_in")
        ex_in = sem("ex_in")
        ex_out = sem("ex_out")
        sum_ready = sem("sum_ready")
        sum_out = [sem(f"sum_out{b}") for b in range(2)]
        tail = sem("tail")
        tail_t = sem("tail_t")
        carry = sem("carry")
        carry_t = sem("carry_t")
        cex_in = sem("cex_in")
        cex_out = sem("cex_out")
        fx_in = sem("fx_in")
        fx_ready = sem("fx_ready")
        fx_out = sem("fx_out")
        ends_in = [sem(f"ends_in{k}") for k in range(2)]
        ends_ready = sem("ends_ready")
        elu_in = sem("elu_in")
        elu_out = sem("elu_out")
        big_zero = sem("big_zero")
        acc_zero = sem("acc_zero")
        src_f_ready = sem("src_f_ready")
        rows_t = sem("rows_t")
        rows_used = sem("rows_used")
        m_done = sem("m_done")
        m_copied = sem("m_copied")
        msg_free = sem("msg_free")
        h_scat = sem("h_scat")
        hi_in = sem("hi_in")
        he_in = [sem(f"he_in{b}") for b in range(2)]
        he_free = sem("he_free")
        ea_in = sem("ea_in")
        ea_free = sem("ea_free")
        xs_in = sem("xs_in")
        xs_ready = sem("xs_ready")
        scat = [sem(f"scat{k}") for k in range(SETS)]
        u_t = sem("u_t")
        u_c = sem("u_c")
        xw_ps = sem("xw_ps")
        xw_c = sem("xw_c")
        xn_ready = sem("xn_ready")
        xn_t = sem("xn_t")
        xn_c = sem("xn_c")
        y_ps = sem("y_ps")
        y_done = sem("y_done")
        out_s = sem("out_s")

        SOFT = [l for l in LAYERS if HEADS_OF[l]]
        TABLED = [CONV1, CONV2, GAT, RGCN]
        W_LOADS = [4, 4, 4, 4, 8]

        def weight_loads(sp, l):
            if l in (CONV1, CONV2):
                k = str(l + 1)
                w = a["L0_gnn_W" + k].rearrange("r i o -> i r o")
                yield w_raw[0:D], w
                yield w_raw[D:P], w
                yield kq[:, :, 0:HEADS], a["L0_gnn_K" + k].rearrange("r o h -> o r h")
                yield kq[:, :, HEADS:2 * HEADS], a["L0_gnn_Q" + k].rearrange("r o h -> o r h")
            elif l == GAT:
                yield w_raw[0:D, 0, :], a["L1_gnn_W"]
                yield w_raw[D:P, 0, :], a["L1_gnn_W"]
                yield kq[:, 0, 0:1], a["L1_gnn_a"][0:D].rearrange("(o h) -> o h", h=1)
                yield kq[:, 0, 1:2], a["L1_gnn_a"][D:2 * D].rearrange("(o h) -> o h", h=1)
            elif l == RGCN:
                w = a["L2_gnn_weight"].rearrange("b i o -> i b o")
                yield w_raw[0:D, 0:4, :], w
                yield w_raw[D:P, 0:4, :], w
                yield w_comp[:, :], a["L2_gnn_w_comp"].rearrange("r b -> (r b)").partition_broadcast(P)
                yield bias[:, 2 * D:3 * D], a["L2_gnn_h_bias"].partition_broadcast(P)
            else:
                yield wide[0:D, 3, :], a["L3_gnn_W1"]
                yield wide[D:P, 3, :], a["L3_gnn_W1"]
                yield wide[:, 4, 0:D], a["L3_gnn_W2"]
                yield wide[:, 4, D:2 * D], a["L3_gnn_b2"].partition_broadcast(P)
                yield wide[:, 0, :], a["L3_gnn_b1"].partition_broadcast(P)
                yield wide[:, 1, :], a["L3_gnn_ln_g"].partition_broadcast(P)
                yield wide[:, 2, :], a["L3_gnn_ln_b"].partition_broadcast(P)
                yield eps1[:, :], a["L3_gnn_eps"].partition_broadcast(P)

        def w_loaded(l):
            return 16 * sum(W_LOADS[:l + 1])

        QZ = EPP * REL * HEADS // (ZREP * ZW)
        assert QZ * ZREP * ZW == EPP * REL * HEADS and ZREP * ZW == J * D and EPP % ZREP == 0
        ZEROS = QZ + 2

        def slots(l):
            h = HEADS_OF[l]
            ri, ro = row_in(l), row_out(l)
            G = cut(0, 2, J, ri)
            O = cut(XI, 2, J, ro)
            return h, G, O

        block = ctx.enter_context(nc.Block())

        @block.sync
        def _(sp):
            part = lambda x: x.rearrange("(p j) -> p j", p=P)
            sp.dma_start(dst_i, part(a["dst"])).then_inc(dst_in, 16)
            sp.wait_ge(memsets, 1)
            sp.dma_start(prev_i[1:P, :], part(a["dst"])[0:P - 1, EPP - 1:EPP]).then_inc(prev_in, 16)
            sp.dma_start(src1[:, 0:EPP], part(a["src"])).then_inc(loaded, 16)
            sp.dma_start(src8[:, 0:EPP], part(a["edge_type_8"])).then_inc(loaded, 16)
            sp.dma_start(X[:, :, :], a["x"].rearrange("(p t) d -> p t d", p=P)).then_inc(loaded, 16)
            sp.dma_start(bias[:, 0:D], a["L0_gnn_b1"].partition_broadcast(P)).then_inc(loaded, 16)
            sp.dma_start(bias[:, D:2 * D], a["L0_gnn_b2"].partition_broadcast(P)).then_inc(loaded, 16)
            for to, of in weight_loads(sp, CONV1):
                sp.dma_start(to, of).then_inc(w_in, 16)
            sp.wait_ge(dst_ready, 1)
            sp.dma_start(dst_f.rearrange("(p s) k -> p (s k)", p=P), dst_v).then_inc(idx_dram, 16)
            sp.dma_start(sub_last, sub_v).then_inc(idx_dram, 16)
            for l in LAYERS:
                if l in TABLED:
                    w = REL_OF[l] * row_in(l)
                    rows = tables[l].rearrange("(p t r) f -> p t (r f)", p=P, t=NT)
                    n0 = NT * l + 2
                    with sp.Fori(0, TURNS) as g:
                        for q in range(GP):
                            sp.wait_ge(free_a, g * GT + (n0 + 2 * q + 2))
                            sp.dma_start(rows[:, bass.ds(g * GT + 2 * q, 2), :], stage[:, q, :, 0:w]).then_inc(stored[q], 16)
                    if l == CONV1:
                        sp.wait_ge(cnt_ready, 1)
                        sp.dma_start(counts[1:NP + 1, :].rearrange("(p t) k -> p (t k)", p=P), ix[:, 5, :]).then_inc(cnt_out, 16)
                        sp.dma_start(counts[0:1, :], ix[0:1, 7, 0:1]).then_inc(cnt_out, 16)
                        sp.wait_ge(cnt_out, 32)
                        sp.dma_start(ix[:, 6, :], counts[0:NP, :].rearrange("(p t) k -> p (t k)", p=P)).then_inc(cnt_in, 16)
                    if l in SOFT:
                        sp.wait_ge(free_a, NT * (l + 1) + 2)
                        k = q_cols(l)
                        sp.dma_start(q_node[l].rearrange("(p t) k -> p (t k)", p=P), Qn[:, 0:NT * k]).then_inc(qn_out, 16)
                else:
                    sp.wait_ge(h_ready, TURNS * (l + 1))
                    sp.dma_start(tables[l].rearrange("(p t) f -> p t f", p=P), H).then_inc(table_out, 16)
                if l < GINE:
                    if l in TABLED:
                        sp.wait_ge(tile_mm, NT * (l + 1))
                    for to, of in weight_loads(sp, l + 1):
                        sp.dma_start(to, of).then_inc(w_in, 16)
                if l in SUMMED:
                    half = ACC_ROWS // P * D // 2
                    if l == CONV1:
                        sp.wait_ge(zeros_out, 16 * ZEROS)
                    for k in range(ACCS // 4 * l, ACCS // 4 * (l + 1)):
                        for c in range(2):
                            sp.dma_start(acc[k].rearrange("(p t) f -> p (t f)", p=P)[:, c * half:(c + 1) * half],
                                         zeros_d[:, 0:half]).then_inc(acc_zero, 16)
                if l == GINE:
                    sp.wait_ge(h_scat, 16 * NT)
                    w = J * D
                    he = h_edge.rearrange("(p j) k -> p (j k)", p=P)
                    ea = a["edge_attr_64"].rearrange("(p j) k -> p (j k)", p=P)
                    with sp.Fori(0, CH // 2) as i:
                        for b in range(2):
                            sp.wait_ge(he_free, i * 2 + (b + 1))
                            sp.dma_start(HE[:, b].rearrange("p j d -> p (j d)"),
                                         he[:, bass.ds(i * (2 * w) + b * w, w)]).then_inc(he_in[b], 16)
                            sp.wait_ge(ea_free, i * 2 + (b + 1))
                            sp.dma_start(EA.rearrange("p j d -> p (j d)"),
                                         ea[:, bass.ds(i * (2 * w) + b * w, w)]).then_inc(ea_in, 16)
                    break
                rows = sums[l].rearrange("(p j) f -> p j f", p=P)
                _, _, O = slots(l)
                with sp.Fori(0, CH // 2) as i:
                    for b in range(2):
                        sp.wait_ge(sum_ready, i * 2 + (CH * l + b + 1))
                        sp.dma_start(rows[:, bass.ds(i * (2 * J) + b * J, J), :], O[:, b]).then_inc(sum_out[b], 16)
                        if l == CONV1:
                            he = h_edge.rearrange("(p j) k -> p (j k)", p=P)
                            sp.dma_start(he[:, bass.ds(i * (2 * J * D) + b * J * D, J * D)], zeros_d).then_inc(big_zero, 16)
            for k in range(SETS):
                sp.wait_ge(scat[k], 16 * CH * J // SETS)
            result_rows = out.rearrange("(p t) d -> p t d", p=P)

            def load_sums(g):
                tiles = bass.ds(g * (GT * D), GT * D)
                sp.wait_ge(ac_free, g + 1)
                for k in range(ACCS):
                    sp.dma_start(AC[:, k, :], acc[k][0:NP, :].rearrange("(p t) f -> p (t f)", p=P)[:, tiles]).then_inc(ac_in, 16)
                sp.dma_start(AC[:, ACCS, :], tables[GINE].rearrange("(p t) f -> p (t f)", p=P)[:, tiles]).then_inc(ac_in, 16)

            def store_result(g):
                sp.wait_ge(y_done, g + 1)
                sp.dma_start(result_rows[:, bass.ds(g * GT, GT), :], X[:, bass.ds(g * GT, GT), :]).then_inc(out_s, 16)

            with sp.Fori(0, 3) as g:
                load_sums(g)
            with sp.Fori(0, TURNS - 3) as g:
                load_sums(g + 3)
                store_result(g)
            with sp.Fori(0, 3) as g:
                store_result(g + (TURNS - 3))
            sp.wait_ge(out_s, 16 * TURNS)

        @block.gpsimd
        def _(pool):
            def gather(to, table, index, s):
                pool.indirect_dma_start(out=to, out_offset=None, in_=table,
                                        in_offset=bass.IndirectOffsetOnAxis(ap=index, axis=0)).then_inc(s, 16)

            pool.memset(ident[:, :], 0.0).then_inc(ident_z, 1)
            pool.wait_ge(ident_z, 1)
            pool.affine_select(out=ident[:, :], in_=ident[:, :], compare_op=ALU.not_equal, fill=1.0, base=0,
                               pattern=[[-1, P]], channel_multiplier=1).then_inc(consts, 1)
            pool.iota(node_i, pattern=[[1, NT]], base=0, channel_multiplier=NT).then_inc(consts, 1)
            pool.iota(iota_i, pattern=[[1, REL]], base=0, channel_multiplier=0).then_inc(consts, 1)
            pool.iota(far_j, pattern=[[1, EPP]], base=-1, channel_multiplier=0,
                      allow_small_or_imprecise_dtypes=True).then_inc(consts, 1)

            pool.iota(idle_i[:, :], pattern=[[1, 1]], base=NP, channel_multiplier=1).then_inc(consts, 1)
            pool.memset(lower[:, :], 1.0).then_inc(ident_z, 1)
            pool.wait_ge(ident_z, 2)
            pool.affine_select(out=lower[:, :], in_=lower[:, :], compare_op=ALU.is_gt, fill=0.0, base=0,
                               pattern=[[-1, P]], channel_multiplier=1).then_inc(consts, 1)
            pool.iota(edge0_i, pattern=[[1, 1]], base=0, channel_multiplier=EPP).then_inc(consts, 1)
            pool.wait_ge(idx_dram, 32)
            for g in range(TURNS):
                pool.wait_ge(search, g + 1)
                for t in range(GT):
                    gather(got_mid[g][:, t, :], sub_last, ix_i[:, 0, GT * g + t:GT * g + t + 1], mid_in[g])
            for g in range(TURNS):
                pool.wait_ge(search, TURNS + g + 1)
                for t in range(GT):
                    gather(got_low[g][:, t, :], dst_f, ix_i[:, 1, GT * g + t:GT * g + t + 1], low_in[g])
            pool.wait_ge(index_done, 1)
            pool.wait_ge(zeros_out, 16 * ZEROS)

            for l in LAYERS:
                if l in SOFT:
                    k = q_cols(l)
                    for t in range(NT):
                        if t % GT == 0:
                            pool.wait_ge(free_a, NT * l + t + GT + 2)
                        pool.indirect_dma_start(
                            out=q_edge[l], out_offset=bass.IndirectOffsetOnAxis(ap=start_i[:, t:t + 1], axis=0),
                            in_=Qn[:, t * k:(t + 1) * k], in_offset=None,
                            bounds_check=EP - 1, oob_is_err=False).then_inc(q_scat, 16)
                    pool.wait_ge(qn_out, 16 * (l + 1))
                    gather(q_init[:, 0:k], q_node[l], first_node[:, 0:1], qi_in)
                if l == GINE:
                    pool.wait_ge(big_zero, 16 * CH)
                    pool.wait_ge(acc_zero, 16 * 2 * ACCS)
                    for t in range(NT):
                        if t % GT == 0:
                            pool.wait_ge(h_ready, TURNS * l + t // GT + 1)
                        pool.indirect_dma_start(
                            out=h_edge, out_offset=bass.IndirectOffsetOnAxis(ap=start_i[:, t:t + 1], axis=0),
                            in_=H[:, t, :], in_offset=None,
                            bounds_check=EP - 1, oob_is_err=False).then_inc(h_scat, 16)
                    pool.wait_ge(table_out, 16)
                    gather(h_ini, tables[GINE], first_node[:, 0:1], hi_in)
                    with pool.Fori(0, CH // GC) as i:
                        for c in range(GC):
                            b = c % 2
                            pool.wait_ge(idx_ready, i * GC + ((CH + 2) * len(SUMMED) + c + 1))
                            pool.sem_inc(chunk_begun, 1)
                            for j in range(J):
                                m, k = (c * J + j) // BATCH, (c * J + j) // BATCH % SETS
                                if j % GROUP == 0:
                                    pool.wait_ge(m_copied, i * (GC * NG) + (NG * c + j // GROUP + 3))
                                    pool.sem_inc(chunk_begun, 1)
                                if j % BATCH == 0:
                                    pool.wait_ge(scat[k], i * (16 * GC * J // SETS) + 16 * BATCH * (m // SETS))
                                    pool.sem_inc(msg_free if j // BATCH == SETS - 1 else chunk_begun, 1)
                                pool.indirect_dma_start(
                                    out=acc[BATCH * k + j % BATCH],
                                    out_offset=bass.IndirectOffsetOnAxis(ap=idx[:, b, j:j + 1], axis=0),
                                    in_=MSG[:, b, j, :], in_offset=None, compute_op=ALU.add).then_inc(scat[k], 16)
                    break
                for q in range(GP):
                    pool.wait_ge(stored[q], 16 * TURNS * (l + 1))
                _, G, _ = slots(l)
                with pool.Fori(0, CH // 2) as i:
                    for b in range(2):
                        pool.wait_ge(idx_ready, i * 2 + ((CH + 2) * l + b + 1))
                        pool.sem_inc(chunk_begun, 1)
                        for j in range(J):
                            gather(G[:, b, j, :], tables[l], idx[:, b, j:j + 1], gathered[l][b])
                for b in range(2):
                    pool.wait_ge(sum_out[b], 16 * (CH // 2) * (l + 1))
                gather(fx[:, 0:row_out(l)], sums[l], fix_i[:, 0:1], fx_in)
                pool.wait_ge(fx_ready, l + 1)
                pool.indirect_dma_start(
                    out=sums[l], out_offset=bass.IndirectOffsetOnAxis(ap=fix_i[:, 0:1], axis=0),
                    in_=fx[:, 0:row_out(l)], in_offset=None).then_inc(fx_out, 16)
                pool.wait_ge(fx_out, 16 * (l + 1))
                for g in range(TURNS + 1):
                    if g < TURNS:
                        for t in range(GT * g, GT * (g + 1)):
                            gather(got[l][:, t, :], sums[l], end_i[:, t:t + 1], ends_in[g % 2])
                    if g:
                        k = (g - 1) % 2
                        landed = (TURNS + 1 - k) // 2 * l + (g - 1) // 2 + 1
                        pool.wait_ge(ends_in[k], 16 * GT * landed)
                        pool.sem_inc(ends_ready, 1)

        @block.scalar
        def _(act):
            steps = Steps(act, act_s)
            act.sem_inc(free_a, 2)
            act.sem_inc(m_copied, 2)
            act.wait_ge(zeroed, 1)
            act.wait_ge(idx_dram, 32)
            act.dma_start(zeros_d.rearrange("p (a w) -> p a w", a=ZREP), bc(zeros, 1, ZREP)).then_inc(zeros_out, 16)
            act.dma_start(q_one.rearrange("(p a j) k -> p a (j k)", p=P, a=ZREP),
                          bc(zeros[:, 0:EPP // ZREP], 1, ZREP)).then_inc(zeros_out, 16)
            in_turn = QZ // TURNS

            def zero_q(part):
                n = ZREP * ZW
                act.dma_start(q_rel.rearrange("(p j) k -> p (j k)", p=P)[:, bass.ds(part * n, n)]
                              .rearrange("p (a w) -> p a w", a=ZREP), bc(zeros, 1, ZREP)).then_inc(zeros_out, 16)

            for c in range(QZ - in_turn * TURNS):
                zero_q(c)

            def std(n):
                act.wait_ge(var_in, n)
                act.activation(st[:, 2, 0:GT], st[:, 1, 0:GT], ACT.Sqrt).then_inc(std_out, 1)

            for l in LAYERS:
                w, k = REL_OF[l] * row_in(l), q_cols(l)
                half = w // 2 if REL_OF[l] > 1 else w
                qn = Qn[:, 0:NT * k].rearrange("p (t k) -> p t k", t=NT) if k else None
                def exponentials(g):
                    if l == RGCN:
                        act.wait_ge(elu_in, g + 1)
                        act.activation(EL, EL, ACT.Exp).then_inc(elu_out, 1)

                def roots(g):
                    if l != CONV2:
                        std(g + TURNS * {CONV1: 0, GAT: 1, RGCN: 2, GINE: 3}[l] + 1)

                def table_turn(g, ahead):
                    def copy_pair(q):
                        act.wait_ge(pair_t, g * GP + (GP * TURNS * l + q + 1))
                        act.copy(h_t[:, q, :], ps[:, q % 2, 0:P]).then_inc(pair_c, 1)

                    if l == CONV1:
                        for c in range(in_turn):
                            zero_q(g * in_turn + (QZ - in_turn * TURNS + c))
                    copy_pair(0)
                    for q in range(GP):
                        if q + 1 < GP:
                            copy_pair(q + 1)
                        if ahead and q == 1:
                            exponentials(g + 1)
                        if ahead and q == 4:
                            roots(g + 1)
                        act.wait_ge(stored[q], g * 16 + 16 * TURNS * l)
                        for u in (2 * q, 2 * q + 1):
                            bank = 2 + 2 * (u % 2)
                            act.wait_ge(tile_mm, g * GT + (NT * l + u + 1))
                            last = act.copy(stage[:, q, u % 2, 0:half], ps[:, bank, 0:half])
                            if half < w:
                                last = act.copy(stage[:, q, u % 2, half:w], ps[:, bank + 1, 0:w - half])
                            if k:
                                last = act.copy(qn[:, bass.ds(g * GT + u, 1), :],
                                                ps[:, bank + 1, w - half:w - half + k].unsqueeze(1))
                            last.then_inc(free_a, 1)

                if l in (CONV1, RGCN):
                    exponentials(0)
                    roots(0)
                    with act.Fori(0, TURNS - 1) as g:
                        table_turn(g, True)
                    table_turn(TURNS - 1, False)
                else:
                    with act.Fori(0, TURNS) as g:
                        roots(g)
                        if l in TABLED:
                            table_turn(g, False)
                h, _, _ = slots(l)
                if h:
                    k = q_cols(l)
                    w = J * k
                    rows = q_edge[l].rearrange("(p j) k -> p (j k)", p=P)
                    to = [cut(at_q + b * w, w) for b in range(2)]
                    nth = l
                    act.wait_ge(q_scat, 16 * NT * (l + 1))
                    ex = cut(at_s + 1000, 2 * h * J)
                    with act.Fori(0, CH // 2) as i:
                        for b in range(2):
                            act.wait_ge(e_free, i * 2 + ((CH + 2) * nth + b + 1))
                            act.dma_start(to[b], rows[:, bass.ds(i * (2 * w) + b * w, w)]).then_inc(e_in[b], 16)
                            act.wait_ge(ex_in, i * 2 + (CH * nth + b + 1))
                            act.activation(ex, ex, ACT.Exp).then_inc(ex_out, 1)
                if l == RGCN:
                    act.wait_ge(ew_free, 1)
                    act.dma_start(cut(at_q, EPP), a["edge_weight1"].rearrange("(p j) k -> p (j k)", p=P)).then_inc(ew_in, 16)
                if h:
                    act.wait_ge(cex_in, 2 * l + 1)
                    act.activation(ex_c[0:D + h], ex_c[0:D + h], ACT.Exp).then_inc(cex_out, 1)
                    act.wait_ge(cex_in, 2 * l + 2)
                    act.activation(fac[:, :, 0:D + h], fac[:, :, 0:D + h], ACT.Exp).then_inc(cex_out, 1)
            with act.Fori(0, CH // 2) as i:
                for b in range(2):
                    act.wait_ge(xs_in, i * 2 + (b + 1))
                    act.activation(XS[:, b], XS[:, b], ACT.Relu).then_inc(xs_ready, 1)
                    act.wait_ge(msg_free, i * 2 + b)
                    for n in range(NG):
                        j0, j1 = GROUP * n, min(GROUP * (n + 1), J)
                        act.wait_ge(m_done, i * (2 * NG) + (NG * b + n + 3))
                        act.copy(MSG[:, b, j0:j1, :],
                                 ps[:, 2 + n % 2, 0:(j1 - j0) * D].rearrange("p (j d) -> p j d", d=D)).then_inc(m_copied, 1)

            def copy_u(g):
                act.wait_ge(u_t, g + 1)
                act.copy(h_t[:, 0:4, :], ps[:, 0, :].rearrange("p (q c) -> p q c", q=4))
                act.copy(h_t[:, 4:GP, :], ps[:, 1, 0:(GP - 4) * P].rearrange("p (q c) -> p q c", c=P)).then_inc(u_c, 1)

            def copy_xn(g):
                std(g + (4 * TURNS + 1))
                act.wait_ge(xn_t, g + 1)
                act.copy(xt[:, 0:8, :], ps[:, 0:2, :].rearrange("p a (u c) -> p (a u) c", c=P))
                act.copy(xt[:, 8:GT, :],
                         ps[:, 6:8, :].rearrange("p a (u c) -> p (a u) c", c=P)[:, 0:GT - 8, :]).then_inc(xn_c, 1)

            copy_u(0)
            with act.Fori(0, TURNS - 1) as g:
                copy_u(g + 1)
                copy_xn(g)
            copy_xn(TURNS - 1)

        @block.tensor
        def _(pe):
            def ps_pair(q):
                return ps[:, q % 2, 0:P]

            pe.sem_inc(m_done, 2)

            def source_rows(i, phase, b, n, src_b):
                pe.wait_ge(rows_used, i * (2 * NG) + (2 * NG * (CH // 2) * phase + NG * b + n + 1))
                for j in range(GROUP * n, min(GROUP * (n + 1), J)):
                    c = j % GROUP
                    last = pe.transpose(ps[:, n % 2, c * P:(c + 1) * P], src_b[:, j:j + 1].to_broadcast([P, P]), ident[:, :])
                last.then_inc(rows_t, 1)

            def prepare(l):
                h = HEADS_OF[l]
                if not h:
                    return
                pe.wait_ge(w_in, w_loaded(l))
                if l > 1:
                    pe.wait_ge(fx_ready, l - 1)
                elif l == 0:
                    pe.wait_ge(banks_read, 1)
                for r in range(REL_OF[l]):
                    last = pe.transpose(ps[0:D, 6 + r // 4, (r % 4) * P:(r % 4 + 1) * P], w_raw[:, r, :], ident[:, :])
                last.then_inc(wt_ps, 1)
                pe.wait_ge(wt_sb, l + 1)
                for r in range(REL_OF[l]):
                    last = pe.matmul(ps[:, 0, r * 2 * h:(r + 1) * 2 * h], w_t[:, r, :], kq[:, r, 0:2 * h],
                                     start=True, stop=True)
                last.then_inc(kq_ps, 1)

            pe.wait_ge(consts, 7)
            pe.wait_ge(top_in, 1)
            pe.transpose(ps[:, 6, 0:P], last_b, ident[:, :]).then_inc(top_out, 1)
            pe.wait_ge(top_in, 2)
            pe.transpose(ps[:, 7, 0:P], cont_b, ident[:, :]).then_inc(top_out, 1)

            for l in LAYERS:
                h = HEADS_OF[l]
                if l == CONV1:
                    prepare(l)
                if l in TABLED:
                    w = REL_OF[l] * row_in(l)
                    half = w // 2 if REL_OF[l] > 1 else w
                    cols = w + q_cols(l)
                    pe.wait_ge(w_done, l + 1)
                    with pe.Fori(0, TURNS) as g:
                        pe.wait_ge(h_ready, g + (TURNS * l + 1))
                        def turn_pair(q):
                            pair = h_s[:, 2 * q:2 * q + 2, :].rearrange("p t d -> p (t d)")
                            pe.transpose(ps_pair(q), pair, ident[:, :]).then_inc(pair_t, 1)

                        turn_pair(0)
                        for q in range(GP):
                            if q + 1 < GP:
                                turn_pair(q + 1)
                            pe.wait_ge(pair_c, g * GP + (GP * TURNS * l + q + 1))
                            for k in range(2):
                                u = 2 * q + k
                                lo = slice(D * k, D * k + D)
                                pe.wait_ge(free_a, g * GT + (NT * l + u + 1))
                                pe.matmul(ps[:, 2 + 2 * k, 0:half], h_t[lo, q, :], w_all[lo, 0:half],
                                          start=True, stop=True)
                                last = pe.matmul(ps[:, 3 + 2 * k, 0:cols - half], h_t[lo, q, :],
                                                 w_all[lo, half:cols], start=True, stop=True)
                                last.then_inc(tile_mm, 1)
                if l + 1 in TABLED:
                    prepare(l + 1)
                if l == RGCN:
                    with pe.Fori(0, CH // 2) as i:
                        for b in range(2):
                            pe.wait_ge(src_f_ready, i * 2 + (b + 1))
                            for n in range(NG):
                                source_rows(i, 0, b, n, first_f[:, b])
                if l == GINE:
                    with pe.Fori(0, CH // 2) as i:
                        for b in range(2):
                            pe.wait_ge(src_f_ready, i * 2 + (CH + b + 1))
                            source_rows(i, 1, b, 0, src_f[:, b])
                            for n in range(NG):
                                if n + 1 < NG:
                                    source_rows(i, 1, b, n + 1, src_f[:, b])
                                if n == 0:
                                    pe.wait_ge(xs_ready, i * 2 + (b + 1))
                                pe.wait_ge(rows_used, i * (2 * NG) + (NG * CH + NG * b + n + 3))
                                pe.wait_ge(m_copied, i * (2 * NG) + (NG * b + n + 1))
                                for j in range(GROUP * n, min(GROUP * (n + 1), J)):
                                    c = j % GROUP
                                    last = pe.matmul(ps[:, 2 + n % 2, c * D:(c + 1) * D], SAME[:, n % 2, c, :],
                                                     XS[:, b, j, :], start=True, stop=True)
                                last.then_inc(m_done, 1)
                    break
                f = D + h
                pe.wait_ge(tail, l + 1)
                if h:
                    pe.transpose(ps[0:f, 6, 0:P], e_m[:, 0:f], ident[:, :])
                pe.transpose(ps[0:f, 6, P:2 * P], e_a[:, 0:f], ident[:, :]).then_inc(tail_t, 1)
                pe.wait_ge(carry, l + 1)
                if h:
                    pe.transpose(ps[:, 7, 0:f], cm[0:f, 0:P], ident[0:f, 0:f])
                pe.transpose(ps[:, 7, P:P + f], ca[0:f, 0:P], ident[0:f, 0:f]).then_inc(carry_t, 1)
            pe.wait_ge(w_in, w_loaded(GINE))

            def first_product(g):
                pe.wait_ge(u_ready, g + 1)
                for q in range(GP):
                    pair = U[:, 2 * q:2 * q + 2, :].rearrange("p t d -> p (t d)")
                    last = pe.transpose(ps[:, q // 4, (q % 4) * P:(q % 4 + 1) * P], pair, ident[:, :])
                last.then_inc(u_t, 1)
                pe.wait_ge(u_c, g + 1)
                for u in range(GT):
                    k, q = u % 2, u // 2
                    lo = slice(D * k, D * k + D)
                    last = pe.matmul(ps[:, 2 + 2 * k + q // 4, (q % 4) * P:(q % 4 + 1) * P], h_t[lo, u // 2, :], wide[lo, 3, :],
                                     start=True, stop=True)
                last.then_inc(xw_ps, 1)

            def second_product(g):
                pe.wait_ge(xn_ready, g + 1)
                for u in range(GT):
                    last = pe.transpose(ps[:, u // 4 if u < 8 else 4 + u // 4, (u % 4) * P:(u % 4 + 1) * P], xr[:, u, :],
                                        ident[:, :])
                last.then_inc(xn_t, 1)
                pe.wait_ge(xn_c, g + 1)
                for u in range(GT):
                    last = pe.matmul(ps[:, 6 + u // 8, (u % 8) * D:(u % 8 + 1) * D], xt[:, u, :], wide[:, 4, 0:D],
                                     start=True, stop=True)
                last.then_inc(y_ps, 1)

            first_product(0)
            with pe.Fori(0, TURNS - 1) as g:
                first_product(g + 1)
                second_product(g)
            second_product(TURNS - 1)

        @block.vector
        def _(dve):
            s = Steps(dve, v)
            done, settle = s.done, s.settle
            tt, ts_, stt = dve.tensor_tensor, dve.tensor_scalar, dve.scalar_tensor_tensor
            dve.sem_inc(rows_used, 2)

            dve.memset(prev_i, -1).then_inc(memsets, 1)
            dve.memset(zeros, 0.0).then_inc(zeroed, 1)
            done(dve.memset(src1[:, EPP:], 0))
            done(dve.memset(src8[:, EPP:], 0))
            done(dve.memset(ix[:, 7, :], 0.0))
            dve.wait_ge(dst_in, 16)
            done(dve.tensor_copy(dst_v, dst_i))
            settle()
            dve.tensor_copy(sub_v, dst_v[:, SUB - 1:EPP:SUB]).then_inc(dst_ready, 1)
            dve.tensor_copy(last_b, dst_v[:, EPP - 1:EPP].to_broadcast([P, P])).then_inc(top_in, 1)
            done(dve.tensor_copy(first_node[:, :], dst_i[:, 0:1]))
            dve.wait_ge(consts, 7)
            done(dve.tensor_copy(ix[:, 0, :], node_i))
            settle()
            done(ts_(ix[:, 0, :], ix[:, 0, :], float(N - 1), None, ALU.min))
            settle()
            dve.wait_ge(top_out, 1)
            for g in range(TURNS):
                tiles = slice(g * GT, (g + 1) * GT)
                done(tt(cmp_top, bc(ps[:, 6, 0:P], 1, GT), bc(ix[:, 0, tiles], 2, P), ALU.is_le))
                settle()
                done(dve.tensor_reduce(ix[:, 1, tiles], cmp_top, AX, ALU.add))
                settle()
                dve.tensor_copy(ix_i[:, 0, tiles], ix[:, 1, tiles]).then_inc(search, 1)
            done(tt(cont[:, 1:EPP], dst_v[:, 1:EPP], dst_v[:, 0:EPP - 1], ALU.is_equal))
            dve.wait_ge(prev_in, 16)
            done(dve.tensor_copy(prev[:, 0:1], prev_i))
            done(dve.tensor_copy(edge0, edge0_i))
            done(dve.tensor_copy(iota_r[:, :], iota_i))
            done(dve.tensor_copy(idle[:, :], idle_i[:, :]))
            settle()
            done(tt(cont[:, 0:1], dst_v[:, 0:1], prev[:, 0:1], ALU.is_equal))
            settle()
            done(dve.tensor_reduce(cont_all[:, :], cont[:, :], AX, ALU.min))
            done(stt(out=far_j[:, 1:EPP], in0=cont[:, 1:EPP], scalar=FAR, in1=far_j[:, 1:EPP], op0=ALU.mult, op1=ALU.add))
            done(ts_(neg0[:, :], cont[:, 0:1], -1.0, BIG, ALU.add, ALU.mult))
            settle()
            done(dve.tensor_reduce(prev[:, 0:1], far_j[:, 1:EPP], AX, ALU.min))
            settle()
            done(ts_(prev[:, 0:1], prev[:, 0:1], float(EPP - 1), None, ALU.min))
            settle()
            done(ts_(fix_i[:, :], prev[:, 0:1], edge0[:, 0:1], None, ALU.add))
            dve.tensor_copy(cont_b, cont_all[:, 0:1].to_broadcast([P, P])).then_inc(top_in, 1)
            dve.wait_ge(loaded, 16 * 5)
            done(dve.tensor_copy(rel[:, :], src8[:, 0:EPP]))
            dve.wait_ge(top_out, 2)
            dve.tensor_copy(cont_t[:, :], ps[:, 7, 0:P]).then_inc(banks_read, 1)
            dve.wait_ge(banks_read, 1)
            done(ts_(neg_t[:, :], cont_t[:, :], -1.0, BIG, ALU.add, ALU.mult))
            done(stt(out=src8[:, 0:EPP], in0=src1[:, 0:EPP], scalar=float(REL), in1=src8[:, 0:EPP], op0=ALU.mult,
                     op1=ALU.add))

            def second_level(g):
                tiles = slice(g * GT, (g + 1) * GT)
                dve.wait_ge(mid_in[g], 16 * GT)
                done(tt(got_mid[g], got_mid[g], bc(ix[:, 0, tiles], 2, NSUB), ALU.is_le))
                settle()
                done(dve.tensor_reduce(ix[:, 2, tiles], got_mid[g], AX, ALU.add))
                settle()
                done(stt(out=ix[:, 3, tiles], in0=ix[:, 1, tiles], scalar=float(NSUB), in1=ix[:, 2, tiles],
                         op0=ALU.mult, op1=ALU.add))
                settle()
                dve.tensor_copy(ix_i[:, 1, tiles], ix[:, 3, tiles]).then_inc(search, 1)

            def third_level():
                for g in range(TURNS):
                    tiles = slice(g * GT, (g + 1) * GT)
                    dve.wait_ge(low_in[g], 16 * GT)
                    done(tt(got_low[g], got_low[g], bc(ix[:, 0, tiles], 2, SUB), ALU.is_le))
                    settle()
                    done(dve.tensor_reduce(ix[:, 4, tiles], got_low[g], AX, ALU.add))
                settle()
                stt(out=ix[:, 5, :], in0=ix[:, 3, :], scalar=float(SUB), in1=ix[:, 4, :], op0=ALU.mult,
                    op1=ALU.add).then_inc(cnt_ready, 1)
                dve.wait_ge(cnt_ready, 1)
                dve.wait_ge(cnt_in, 16)
                done(tt(mask[:, :], ix[:, 5, :], ix[:, 6, :], ALU.is_gt))
                done(ts_(end_i[:, :], ix[:, 5, :], -1.0, 0.0, ALU.add, ALU.max))
                settle()
                done(ts_(ix[:, 4, :], mask[:, :], -FAR, FAR, ALU.mult, ALU.add))
                settle()
                tt(start_i[:, :], ix[:, 6, :], ix[:, 4, :], ALU.add).then_inc(index_done, 1)
                dve.wait_ge(index_done, 1)

            def norm(src, to, sq, width, nth_std):
                mean, var, sd, rs = (st[:, k, 0:GT] for k in range(4))
                done(dve.tensor_reduce(mean, src, AX, ALU.add))
                settle()
                done(ts_(mean, mean, 1.0 / width, None, ALU.mult))
                settle()
                done(tt(to, src, bc(mean, 2, width), ALU.subtract))
                settle()
                done(tt(sq, to, to, ALU.mult))
                settle()
                done(dve.tensor_reduce(var, sq, AX, ALU.add))
                settle()
                ts_(var, var, 1.0 / width, LN_EPS, ALU.mult, ALU.add).then_inc(var_in, 1)
                dve.wait_ge(std_out, nth_std)
                done(dve.reciprocal(rs, sd))
                settle()
                return rs

            def weights(l):
                h = HEADS_OF[l]
                ri, k, rels = row_in(l), q_cols(l), REL_OF[l]
                w = rels * ri
                dve.wait_ge(w_in, w_loaded(l))
                if h:
                    dve.wait_ge(wt_ps, l + 1)
                    for r0 in range(0, rels, 4):
                        n = min(4, rels - r0)
                        last = dve.tensor_copy(w_t[:, r0:r0 + n, :],
                                               ps[0:D, 6 + r0 // 4, 0:n * P].rearrange("p (r i) -> p r i", r=n))
                    last.then_inc(wt_sb, 1)
                    tab = w_all[:, 0:w].rearrange("p (r f) -> p r f", r=rels)
                    done(dve.tensor_copy(tab[:, :, 0:D], w_raw[:, 0:rels, :]))
                    dve.wait_ge(kq_ps, l + 1)
                    both = ps[:, 0, 0:rels * 2 * h].rearrange("p (r f) -> p r f", r=rels)
                    done(dve.tensor_copy(tab[:, :, D:ri], both[:, :, 0:h]))
                    dve.tensor_copy(w_all[:, w:w + k].rearrange("p (r f) -> p r f", r=rels),
                                    both[:, :, h:2 * h]).then_inc(w_done, 1)
                else:
                    for r in range(rels):
                        o = w_all[:, r * D:(r + 1) * D]
                        done(ts_(o, w_raw[:, 0, :], w_comp[:, 4 * r:4 * r + 1], None, ALU.mult))
                    for b in range(1, 4):
                        settle()
                        for r in range(rels):
                            o = w_all[:, r * D:(r + 1) * D]
                            last = stt(out=o, in0=w_raw[:, b, :], scalar=w_comp[:, 4 * r + b:4 * r + b + 1], in1=o,
                                       op0=ALU.mult, op1=ALU.add)
                            if (b, r) != (3, rels - 1):
                                done(last)
                    last.then_inc(w_done, 1)

            def result(l, g):
                h = HEADS_OF[l]
                tiles = bass.ds(g * GT, GT)
                xg, mk = X[:, tiles, :], mask[:, tiles]
                dve.wait_ge(ends_ready, g + (TURNS * l + 1))
                if h:
                    den = DN[:, :, 0:h]
                    done(ts_(den, got[l][:, tiles, D:D + h], 0.0 if l == GAT else 1e-16, None, ALU.add))
                    settle()
                    done(dve.reciprocal(den, den))
                    settle()
                    done(tt(den, den, bc(mk, 2, h), ALU.mult))
                    settle()
                    w = D // h
                    for hh in range(h):
                        last = tt(Y[:, :, hh * w:(hh + 1) * w], got[l][:, tiles, hh * w:(hh + 1) * w],
                                  bc(den[:, :, hh], 2, w), ALU.mult)
                    done(last)
                else:
                    done(tt(Y, got[l][:, tiles, 0:D], bc(mk, 2, D), ALU.mult))
                settle()
                if l == CONV1:
                    done(tt(Y, Y, bc(bias[:, 0:D], 1, GT), ALU.add))
                    settle()
                    dve.wait_ge(pair_t, g * GP + GP * TURNS * (l + 1))
                    ts_(h_s, Y, 0.0, None, ALU.max).then_inc(h_ready, 1)
                elif l == CONV2:
                    done(tt(Y, Y, bc(bias[:, D:2 * D], 1, GT), ALU.add))
                    settle()
                    done(tt(xg, xg, Y, ALU.add))
                elif l == GAT:
                    ts_(EL, Y, 0.0, None, ALU.min).then_inc(elu_in, 1)
                    dve.wait_ge(elu_out, g + 1)
                    done(stt(out=Y, in0=Y, scalar=0.0, in1=EL, op0=ALU.max, op1=ALU.add))
                    settle()
                    done(stt(out=xg, in0=Y, scalar=-1.0, in1=xg, op0=ALU.add, op1=ALU.add))
                else:
                    done(tt(Y, Y, bc(bias[:, 2 * D:3 * D], 1, GT), ALU.add))
                    settle()
                    done(stt(out=xg, in0=Y, scalar=0.0, in1=xg, op0=ALU.max, op1=ALU.add))
                settle()

            def gine_edges():
                dve.sem_inc(he_free, 2)
                dve.sem_inc(ea_free, 1)
                dve.wait_ge(hi_in, 16)
                with s.loop(CH // 2, 4) as i:
                    for b in range(2):
                        at = i * (2 * J) + b * J
                        cj = cont[:, bass.ds(at, J)]
                        dve.wait_ge(msg_free, i * 2 + b)
                        dve.tensor_copy(src_f[:, b, :], src1[:, bass.ds(at, J)]).then_inc(src_f_ready, 1)
                        dve.tensor_copy(idx[:, b, :], src8[:, bass.ds(at, J)]).then_inc(idx_ready, 1)
                        dve.wait_ge(he_in[b], i * 16 + 16)
                        for f in range(D):
                            last = dve.tensor_tensor_scan(XS[:, b, :, f], cj, HE[:, b, :, f], h_ini[:, f:f + 1],
                                                          ALU.mult, ALU.add)
                        done(last)
                        settle()
                        done(dve.tensor_copy(h_ini, XS[:, b, J - 1, :]))
                        settle()
                        dve.wait_ge(ea_in, i * 32 + 16 * (b + 1))
                        tt(XS[:, b], XS[:, b], EA, ALU.add).then_inc(xs_in, 1)
                        dve.wait_ge(xs_in, i * 2 + (b + 1))
                        dve.sem_inc(ea_free, 1)
                        for n in range(NG):
                            if n == NG // 2:
                                dve.sem_inc(he_free, 1)
                            j0, j1 = GROUP * n, min(GROUP * (n + 1), J)
                            dve.wait_ge(rows_t, i * (2 * NG) + (NG * CH + NG * b + n + 1))
                            dve.wait_ge(m_done, i * (2 * NG) + (NG * b + n + 1))
                            tt(SAME[:, n % 2, 0:j1 - j0, :],
                               ps[:, n % 2, 0:(j1 - j0) * P].rearrange("p (j i) -> p j i", i=P),
                               bc(src_f[:, b, j0:j1], 2, P), ALU.is_equal).then_inc(rows_used, 1)

            def gine_nodes():
                def gine_sum(g):
                    dve.wait_ge(ac_in, g * (16 * (ACCS + 1)) + 16 * (ACCS + 1))
                    n = ACCS // 2
                    while n:
                        done(tt(AC[:, 0:n, :], AC[:, 0:n, :], AC[:, n:2 * n, :], ALU.add))
                        settle()
                        n //= 2
                    dve.wait_ge(u_t, g)
                    stt(out=U.rearrange("p t d -> p (t d)"), in0=AC[:, ACCS, :], scalar=eps1[:, 0:1], in1=AC[:, 0, :],
                        op0=ALU.mult, op1=ALU.add).then_inc(u_ready, 1)
                    dve.wait_ge(u_ready, g + 1)
                    dve.sem_inc(ac_free, 1)

                def add_result(g):
                    dve.wait_ge(y_ps, g + 1)
                    xg = X[:, bass.ds(g * GT, GT), :]
                    xa, xb = X[:, bass.ds(g * GT, 8), :], X[:, bass.ds(g * GT + 8, GT - 8), :]
                    done(tt(xg, xg, bc(wide[:, 4, D:2 * D], 1, GT), ALU.add))
                    settle()
                    done(tt(xa, xa, ps[:, 6, :].rearrange("p (u c) -> p u c", c=D), ALU.add))
                    tt(xb, xb, ps[:, 7, 0:(GT - 8) * D].rearrange("p (u c) -> p u c", c=D), ALU.add).then_inc(y_done, 1)

                def gine_turn(g, first=False, last=False):
                    dve.wait_ge(xw_ps, g + 1)
                    for k in range(2):
                        half_ps = ps[:, 2 + 2 * k:4 + 2 * k, :].rearrange("p a (u c) -> p (a u) c", c=P)[:, 0:GP, :]
                        done(tt(xw[:, k:GT:2, :], half_ps, bc(wide[:, 0, :], 1, GP), ALU.add))
                    settle()
                    if not last:
                        gine_sum(g + 1)
                    if not first:
                        add_result(g - 1)
                    rs = norm(xw, xw, xsq, 2 * D, g + (4 * TURNS + 1))
                    done(tt(xw, xw, bc(rs, 2, 2 * D), ALU.mult))
                    settle()
                    done(tt(xw, xw, bc(wide[:, 1, :], 1, GT), ALU.mult))
                    settle()
                    done(tt(xw, xw, bc(wide[:, 2, :], 1, GT), ALU.add))
                    settle()
                    ts_(xr, xw, 0.0, None, ALU.max).then_inc(xn_ready, 1)
                    dve.wait_ge(xn_ready, g + 1)

                for k in range(SETS):
                    dve.wait_ge(scat[k], 16 * CH * J // SETS)
                dve.sem_inc(ac_free, 1)
                done(ts_(eps1[:, :], eps1[:, :], 1.0, None, ALU.add))
                settle()
                gine_sum(0)
                gine_turn(0, first=True)
                with s.loop(TURNS - 2, 2 + ACCS.bit_length() - 1 + 2 + 6 + 3) as i:
                    gine_turn(i + 1)
                gine_turn(TURNS - 1, last=True)
                add_result(TURNS - 1)

            for l in LAYERS:
                h, G, O = slots(l)
                ri, ro, k = row_in(l), row_out(l), q_cols(l)
                rels = REL_OF[l]
                w = rels * ri
                if l == CONV1:
                    weights(l)
                nth_ln = {CONV1: 0, CONV2: 0, GAT: 1, RGCN: 2, GINE: 3}[l]

                def node_turn(g, tiles):
                    if l:
                        result(l - 1, g)
                    if l != CONV2:
                        dve.sem_inc(x_final, 1)
                        rs = norm(X[:, tiles, :], Y, SQ, D, g + (TURNS * nth_ln + 1))
                        if l in TABLED:
                            dve.wait_ge(pair_t, g * GP + GP * TURNS * l)
                            to = h_s
                        else:
                            to = H[:, tiles, :]
                        stt(out=to, in0=Y, scalar=0.0, in1=bc(rs, 2, D), op0=ALU.max, op1=ALU.mult).then_inc(h_ready, 1)
                    dve.wait_ge(h_ready, g + (TURNS * l + 1))

                if l == CONV1:
                    for g in range(TURNS):
                        node_turn(g, slice(g * GT, (g + 1) * GT))
                        second_level(g)
                    third_level()
                else:
                    with s.loop(TURNS, {CONV2: 5, GAT: 12, RGCN: 12, GINE: 9}[l]) as g:
                        node_turn(g, bass.ds(g * GT, GT))
                if l in TABLED:
                    for q in range(GP):
                        dve.wait_ge(stored[q], 16 * TURNS * (l + 1))
                    dve.wait_ge(free_a, NT * (l + 1) + 2)
                else:
                    dve.wait_ge(table_out, 16)
                    dve.wait_ge(h_scat, 16 * NT)
                    gine_edges()
                    gine_nodes()
                    break
                if h:
                    dve.wait_ge(q_scat, 16 * NT * (l + 1))
                    dve.wait_ge(qn_out, 16 * (l + 1))
                    dve.wait_ge(qi_in, 16 * (l + 1))
                which = src8 if rels > 1 else src1
                nth = l
                ew = cut(at_q, EPP)
                if l == RGCN:
                    dve.sem_inc(ew_free, 1)
                for b in range(2):
                    dve.tensor_copy(idx[:, b, :], which[:, b * J:(b + 1) * J]).then_inc(idx_ready, 1)
                done(dve.memset(O[:, 1, J - 1, :], 0.0))
                if h:
                    dve.sem_inc(e_free, 2)
                    w_e = J * k
                    EQ = [cut(at_q + b * w_e, J, k) for b in range(2)]
                    QX = cut(at_q + 2 * w_e, J, k)
                    TM = cut(at_q + 3 * w_e, J, k)
                    OH = cut(at_s, J, REL)
                    Q = cut(at_s + 500, h, J)
                    M = cut(at_s + 1500, 2, h, J + 1)
                    EX = cut(at_s + 1000, 2, h, J)
                    NEG = cut(at_s + 2010, J)
                    done(dve.memset(M[:, 1, :, J:J + 1], -BIG))
                    done(dve.tensor_copy(QX[:, J - 1, :], q_init[:, 0:k]))
                if l + 1 in TABLED:
                    weights(l + 1)
                if l == RGCN:
                    dve.wait_ge(ew_in, 16)
                per = {CONV1: 24, CONV2: 24, GAT: 18, RGCN: 10}[l]
                settle()
                with s.loop(CH // 2, per) as i:
                    for b in range(2):
                        at = i * (2 * J) + b * J
                        cj = cont[:, bass.ds(at, J)]
                        ob = 1 - b
                        if h:
                            dve.wait_ge(e_in[b], i * 16 + 16 * (CH // 2) * nth + 16)
                            for c in range(k):
                                last = dve.tensor_tensor_scan(TM[:, :, c], cj, EQ[b][:, :, c], QX[:, J - 1, c:c + 1],
                                                              ALU.mult, ALU.add)
                            last.then_inc(e_free, 1)
                            dve.wait_ge(e_free, i * 2 + ((CH + 2) * nth + b + 3))
                            done(dve.tensor_copy(QX[:, J - 1, :], TM[:, J - 1, :]))
                            done(ts_(NEG, cj, -1.0, BIG, ALU.add, ALU.mult))
                            if rels > 1:
                                done(tt(OH, bc(rel[:, bass.ds(at, J)], 2, REL), bc(iota_r[:, :], 1, J), ALU.is_equal))
                                settle()
                                tm4 = TM.rearrange("p j (r h) -> p j h r", r=rels)
                                for hh in range(h):
                                    last = tt(tm4[:, :, hh, :], tm4[:, :, hh, :], OH, ALU.mult)
                                done(last)
                                settle()
                                done(dve.tensor_reduce(Q.rearrange("p h j -> p j h"), tm4, AX, ALU.add))
                                settle()
                                qv = Q
                            else:
                                qv = TM.rearrange("p j k -> p k j")
                                settle()
                            dve.wait_ge(gathered[l][b], i * (16 * J) + 16 * J)
                            done(tt(Q, qv, G[:, b, :, D:ri].rearrange("p j h -> p h j"), ALU.add))
                            settle()
                            done(stt(out=Q, in0=Q, scalar=SLOPE, in1=Q, op0=ALU.mult, op1=ALU.max))
                            done(dve.tensor_copy(M[:, b, :, 0:1], M[:, ob, :, J:J + 1]))
                            settle()
                            for hh in range(h):
                                last = dve.tensor_tensor_scan(M[:, b, hh, 1:J + 1], NEG, Q[:, hh, :],
                                                              M[:, b, hh, 0:1], ALU.add, ALU.max)
                            done(last)
                            settle()
                            done(tt(EX[:, 0], M[:, b, :, 0:J], M[:, b, :, 1:J + 1], ALU.subtract))
                            settle()
                            done(tt(EX[:, 0], EX[:, 0], bc(NEG, 1, h), ALU.add))
                            tt(EX[:, 1], Q, M[:, b, :, 1:J + 1], ALU.subtract).then_inc(ex_in, 1)
                            dve.wait_ge(ex_out, i * 2 + (CH * nth + b + 1))
                            gh = G[:, b, :, 0:D].rearrange("p j (h f) -> p j h f", h=h)
                            for hh in range(h):
                                last = tt(gh[:, :, hh, :], gh[:, :, hh, :], bc(EX[:, 1, hh, :], 2, D // h), ALU.mult)
                            done(last)
                        else:
                            dve.tensor_copy(first_f[:, b, :], src1[:, bass.ds(at, J)]).then_inc(src_f_ready, 1)
                            for n in range(NG):
                                dve.wait_ge(rows_t, i * (2 * NG) + (NG * b + n + 1))
                                for j in range(GROUP * n, min(GROUP * (n + 1), J)):
                                    c = j % GROUP
                                    last = stt(out=junk[:, j, :], in0=ps[:, n % 2, c * P:(c + 1) * P],
                                               scalar=first_f[:, b, j:j + 1], in1=lower[:, :], op0=ALU.is_equal,
                                               op1=ALU.mult, accum_out=before[:, j:j + 1])
                                last.then_inc(rows_used, 1)
                            dve.wait_ge(rows_used, i * (2 * NG) + (NG * b + NG + 2))
                            done(ts_(before, before, 1.0, None, ALU.min))
                            done(ts_(other, first_f[:, b, :], -1.0, idle[:, 0:1], ALU.mult, ALU.add))
                            settle()
                            done(tt(other, other, before, ALU.mult))
                            settle()
                            done(tt(src8[:, bass.ds(at, J)], other, first_f[:, b, :], ALU.add))
                            dve.wait_ge(gathered[l][b], i * (16 * J) + 16 * J)
                            g_b = G[:, b, :, :]
                            done(tt(g_b, g_b, bc(ew[:, bass.ds(at, J)], 2, D), ALU.mult))
                        settle()
                        dve.wait_ge(sum_out[b], i * 16 + 16 * (CH // 2) * l)
                        for f in range(D):
                            fac_j = EX[:, 0, f * h // D, :] if h else cj
                            last = dve.tensor_tensor_scan(O[:, b, :, f], fac_j, G[:, b, :, f], O[:, ob, J - 1, f:f + 1],
                                                          ALU.mult, ALU.add)
                        if h:
                            for hh in range(h):
                                dve.tensor_tensor_scan(O[:, b, :, D + hh], EX[:, 0, hh, :], EX[:, 1, hh, :],
                                                       O[:, ob, J - 1, D + hh:D + hh + 1], ALU.mult, ALU.add)
                            last = dve.tensor_copy(O[:, b, :, D + h:D + 2 * h].rearrange("p j h -> p h j"),
                                                   M[:, b, :, 1:J + 1])
                        last.then_inc(sum_ready, 1)
                        dve.wait_ge(sum_ready, i * 2 + (CH * l + b + 1))
                        dve.tensor_copy(idx[:, b, :], which[:, bass.ds(at + 2 * J, J)]).then_inc(idx_ready, 1)
                f = D + h
                tail_row = O[:, 1, J - 1, :]
                if h:
                    for hh in range(h):
                        done(dve.tensor_copy(e_m[:, hh * D // h:(hh + 1) * D // h],
                                             tail_row[:, f + hh:f + hh + 1].to_broadcast([P, D // h])))
                    done(dve.tensor_copy(e_m[:, D:f], tail_row[:, f:f + h]))
                dve.tensor_copy(e_a[:, 0:f], tail_row[:, 0:f]).then_inc(tail, 1)
                if h:
                    done(dve.memset(cm[:, 0:1], -BIG))
                done(dve.memset(ca[:, 0:1], 0.0))
                dve.wait_ge(tail_t, l + 1)
                settle()
                if h:
                    done(dve.tensor_tensor_scan(cm[0:f, 1:P + 1], neg_t[0:f, :], ps[0:f, 6, 0:P], -BIG, ALU.add, ALU.max))
                    settle()
                    done(tt(ex_c[0:f, 0], cm[0:f, 0:P], cm[0:f, 1:P + 1], ALU.subtract))
                    settle()
                    done(tt(ex_c[0:f, 0], ex_c[0:f, 0], neg_t[0:f, :], ALU.add))
                    tt(ex_c[0:f, 1], ps[0:f, 6, 0:P], cm[0:f, 1:P + 1], ALU.subtract).then_inc(cex_in, 1)
                    dve.wait_ge(cex_out, 2 * l + 1)
                    done(tt(ex_c[0:f, 1], ex_c[0:f, 1], ps[0:f, 6, P:2 * P], ALU.mult))
                    settle()
                    dve.tensor_tensor_scan(ca[0:f, 1:P + 1], ex_c[0:f, 0], ex_c[0:f, 1], 0.0,
                                           ALU.mult, ALU.add).then_inc(carry, 1)
                else:
                    dve.tensor_tensor_scan(ca[0:f, 1:P + 1], cont_t[0:f, :], ps[0:f, 6, P:2 * P], 0.0,
                                           ALU.mult, ALU.add).then_inc(carry, 1)
                dve.wait_ge(carry_t, l + 1)
                dve.wait_ge(fx_in, 16 * (l + 1))
                if h:
                    done(ts_(min_c[:, 0:f], ps[:, 7, 0:f], neg0[:, 0:1], None, ALU.add))
                    for hh in range(h):
                        done(dve.tensor_copy(e_m[:, hh * D // h:(hh + 1) * D // h],
                                             fx[:, f + hh:f + hh + 1].to_broadcast([P, D // h])))
                    done(dve.tensor_copy(e_m[:, D:f], fx[:, f:f + h]))
                    settle()
                    done(tt(mt_c[:, 0:f], e_m[:, 0:f], min_c[:, 0:f], ALU.max))
                    settle()
                    done(tt(fac[:, 0, 0:f], e_m[:, 0:f], mt_c[:, 0:f], ALU.subtract))
                    tt(fac[:, 1, 0:f], min_c[:, 0:f], mt_c[:, 0:f], ALU.subtract).then_inc(cex_in, 1)
                    dve.wait_ge(cex_out, 2 * l + 2)
                    done(tt(fx[:, 0:f], fx[:, 0:f], fac[:, 0, 0:f], ALU.mult))
                    done(tt(ca_b[:, 0:f], ps[:, 7, P:P + f], fac[:, 1, 0:f], ALU.mult))
                    done(dve.tensor_copy(fx[:, f:f + h], mt_c[:, D:f]))
                    settle()
                    tt(fx[:, 0:f], fx[:, 0:f], ca_b[:, 0:f], ALU.add).then_inc(fx_ready, 1)
                else:
                    stt(out=fx[:, 0:D], in0=ps[:, 7, P:P + D], scalar=cont[:, 0:1], in1=fx[:, 0:D],
                        op0=ALU.mult, op1=ALU.add).then_inc(fx_ready, 1)


_INS = ['x', 'src', 'dst', 'edge_attr_64', 'edge_type_8', 'edge_weight1', 'L0_gnn_W1', 'L0_gnn_Q1', 'L0_gnn_K1',
        'L0_gnn_b1', 'L0_gnn_W2', 'L0_gnn_Q2', 'L0_gnn_K2', 'L0_gnn_b2', 'L1_gnn_W', 'L1_gnn_a', 'L2_gnn_weight',
        'L2_gnn_w_comp', 'L2_gnn_h_bias', 'L3_gnn_W1', 'L3_gnn_b1', 'L3_gnn_ln_g', 'L3_gnn_ln_b', 'L3_gnn_W2',
        'L3_gnn_b2', 'L3_gnn_eps']


def kernel(**inputs):
    import concourse.bacc as bacc
    from concourse.bass_utils import run_bass_kernel_spmd as run

    pads = {'x': (NP, 0), 'src': (EP, N), 'dst': (EP, N), 'edge_attr_64': (EP, 0), 'edge_type_8': (EP, 0),
            'edge_weight1': (EP, 0)}
    nc = bacc.Bacc("TRN2", target_bir_lowering=False, num_devices=1)
    arrays, args = {}, {}
    for name in _INS:
        v = np.ascontiguousarray(inputs[name])
        if name in pads:
            rows, fill = pads[name]
            v = np.concatenate([v, np.full((rows - v.shape[0],) + v.shape[1:], fill, v.dtype)])
        arrays[f"in_{name}"] = v
        args[name] = nc.dram_tensor(f"in_{name}", v.shape, mybir.dt.from_np(v.dtype), kind="ExternalInput").ap()
    out = nc.dram_tensor("out", (NP, D), F32, kind="ExternalOutput").ap()
    build(nc, args, out)
    r = run(nc, [arrays], core_ids=[0])
    return r.results[0]["out"][:N]
```
